# Optimizing a Trainium2 kernel written in Bass

```python
import numpy as np
import jax
import jax.numpy as jnp

def _softmax(x, axis=-1):
    return jax.nn.softmax(x, axis=axis)
def _gelu(x):
    return jax.nn.gelu(x, approximate=True)
def _silu(x):
    return jax.nn.silu(x)
def _sigmoid(x):
    return jax.nn.sigmoid(x)
def _layernorm(x, axis=-1, eps=1e-5):
    m = jnp.mean(x, axis=axis, keepdims=True)
    v = jnp.var(x, axis=axis, keepdims=True)
    return (x - m) / jnp.sqrt(v + eps)
def _scatter_add(tgt, idx, src, axis=0):
    return tgt.at[idx].add(src)
def _segment_sum(src, seg, n):
    return jax.ops.segment_sum(src, seg, n)

kernel_name = 'mk_conv_seq_d1_conv_nchw512_abba49'

def setup_inputs(seed: int = 0):
    np.random.seed(seed)
    _w = jnp.asarray
    def _rec_inputs():
        import jax
        import jax.numpy as jnp
        _gk = jax.random.key(seed)
        x = 7.22e-05 + 1 * jax.random.normal(jax.random.fold_in(_gk, 1), (16, 512, 32, 32), jnp.float32)
        return x
    x = _rec_inputs()
    def _L0_conv_setup():
        import jax, jax.numpy as jnp
        import numpy as np
        import math
        B, C, H, W = (16, 512, 32, 32)
        GROUPS = 32
        EPS = 1e-05

        def group_norm(x, w, b):
            Bx, Cx, Hx, Wx = x.shape
            xg = x.reshape(Bx, GROUPS, Cx // GROUPS, Hx, Wx)
            mean = xg.mean(axis=(2, 3, 4), keepdims=True)
            var = xg.var(axis=(2, 3, 4), keepdims=True)
            xg = (xg - mean) * jax.lax.rsqrt(var + EPS)
            xn = xg.reshape(Bx, Cx, Hx, Wx)
            return xn * w[None, :, None, None] + b[None, :, None, None]
        key = jax.random.key(seed)
        ks = jax.random.split(key, 4)
        x = jax.random.normal(ks[0], (B, C, H, W), dtype=jnp.float32)
        gn_w = jnp.ones((C,), dtype=jnp.float32)
        gn_b = jnp.zeros((C,), dtype=jnp.float32)
        qkv_w = jax.random.normal(ks[1], (3 * C, C), dtype=jnp.float32) * (1.0 / math.sqrt(C))
        qkv_b = jnp.zeros((3 * C,), dtype=jnp.float32)
        out_w = jax.random.normal(ks[2], (C, C), dtype=jnp.float32) * (1.0 / math.sqrt(C))
        out_b = jnp.zeros((C,), dtype=jnp.float32)
        return {'x': x, 'gn_w': gn_w, 'gn_b': gn_b, 'qkv_w': qkv_w, 'qkv_b': qkv_b, 'out_w': out_w, 'out_b': out_b}
    _L0_conv_all = _L0_conv_setup()
    _L0_conv_in = {k: v for k, v in _L0_conv_all.items() if k in ('gn_w', 'gn_b', 'qkv_w', 'qkv_b', 'out_w', 'out_b', )}
    del _L0_conv_all

    return {
        "x": x,
        "L0_conv_gn_w": _L0_conv_in["gn_w"],
        "L0_conv_gn_b": _L0_conv_in["gn_b"],
        "L0_conv_qkv_w": _L0_conv_in["qkv_w"],
        "L0_conv_qkv_b": _L0_conv_in["qkv_b"],
        "L0_conv_out_w": _L0_conv_in["out_w"],
        "L0_conv_out_b": _L0_conv_in["out_b"],
    }

def reference(x, L0_conv_gn_w, L0_conv_gn_b, L0_conv_qkv_w, L0_conv_qkv_b, L0_conv_out_w, L0_conv_out_b):
    import jax
    import jax.numpy as jnp
    def _L0_conv_ref(x, gn_w, gn_b, qkv_w, qkv_b, out_w, out_b):
        import jax, jax.numpy as jnp
        import numpy as np
        import math
        B, C, H, W = (16, 512, 32, 32)
        GROUPS = 32
        EPS = 1e-05

        def group_norm(x, w, b):
            Bx, Cx, Hx, Wx = x.shape
            xg = x.reshape(Bx, GROUPS, Cx // GROUPS, Hx, Wx)
            mean = xg.mean(axis=(2, 3, 4), keepdims=True)
            var = xg.var(axis=(2, 3, 4), keepdims=True)
            xg = (xg - mean) * jax.lax.rsqrt(var + EPS)
            xn = xg.reshape(Bx, Cx, Hx, Wx)
            return xn * w[None, :, None, None] + b[None, :, None, None]
        Bx, Cx, Hx, Wx = x.shape
        N = Hx * Wx
        h = group_norm(x, gn_w, gn_b)
        hf = h.reshape(Bx, Cx, N)
        qkv = jnp.einsum('oc,bcn->bon', qkv_w, hf) + qkv_b[None, :, None]
        q, k, v = jnp.split(qkv, 3, axis=1)
        q = q.transpose(0, 2, 1)
        v = v.transpose(0, 2, 1)
        scale = 1.0 / math.sqrt(Cx)
        attn = jnp.einsum('bnc,bcm->bnm', q, k) * scale
        attn = jax.nn.softmax(attn, axis=-1)
        o = jnp.einsum('bnm,bmc->bnc', attn, v)
        o = o.transpose(0, 2, 1)
        o = jnp.einsum('oc,bcn->bon', out_w, o) + out_b[None, :, None]
        return x + o.reshape(Bx, Cx, Hx, Wx)

    def _gn(v, G=32, eps=1e-5):
        B_, C_, H_, W_ = v.shape
        g = v.reshape(B_, G, C_ // G, H_, W_)
        m = jnp.mean(g, axis=(2, 3, 4), keepdims=True)
        s = jnp.var(g, axis=(2, 3, 4), keepdims=True)
        return ((g - m) / jnp.sqrt(s + eps)).reshape(v.shape)

    def _ln_c(v, eps=1e-6):
        m = jnp.mean(v, axis=1, keepdims=True)
        s = jnp.var(v, axis=1, keepdims=True)
        return (v - m) / jnp.sqrt(s + eps)

    def _ln_t(v, eps=1e-5):
        m = jnp.mean(v, axis=-1, keepdims=True)
        s = jnp.var(v, axis=-1, keepdims=True)
        return (v - m) / jnp.sqrt(s + eps)

    def _to_tokens(v):
        B_, C_, H_, W_ = v.shape
        return v.reshape(B_, C_, H_ * W_).transpose(0, 2, 1)
    def _from_tokens(t, like):
        B_, C_, H_, W_ = like.shape
        return t.transpose(0, 2, 1).reshape(B_, C_, H_, W_)

    x = _L0_conv_ref(x, L0_conv_gn_w, L0_conv_gn_b, L0_conv_qkv_w, L0_conv_qkv_b, L0_conv_out_w, L0_conv_out_b)
    return x


_drawn_inputs = setup_inputs


def setup_inputs(seed=0):
    import zlib

    import numpy as np

    out = dict(_drawn_inputs(seed))
    spreads = {'L0_conv_gn_w': (1.0, 0.6),
     'L0_conv_gn_b': (0.0, 0.1),
     'L0_conv_qkv_b': (0.0, 0.1),
     'L0_conv_out_b': (0.0, 0.1)}
    factors = {}
    for name, (base, spread) in spreads.items():
        noise = np.random.default_rng([zlib.crc32(name.encode()), seed]).standard_normal(out[name].shape)
        drawn = base * np.exp(spread * noise) if base else spread * noise
        out[name] = jnp.asarray(drawn.astype(out[name].dtype))
    for name, factor in factors.items():
        out[name] = (out[name] * factor).astype(out[name].dtype)
    return out
```

```python
from contextlib import ExitStack

import numpy as np

import concourse.bass as bass
from concourse import mybir


FP32 = mybir.dt.float32
FP32R = mybir.dt.float32r
ALU = mybir.AluOpType
ACT = mybir.ActivationFunctionType
AX = mybir.AxisListType

P = 128
B, C, H, W = 16, 512, 32, 32
N = H * W
GROUPS = 32
EPS = 1e-5
SCALE = 1.0 / float(C) ** 0.5
CT = C // P
MT = N // P
HALF = 512
NB = N // HALF
RING = 3
UNITS = NB * CT + MT + NB * MT
DMA = 16

T0 = 0
S0 = T0 + NB * CT
V0 = S0 + MT
S1 = V0 + MT
SCORES = (S0, S1)
BQ, BK, BV, GW, GB, BO = (CT * i for i in range(6))


def attention_kernel(nc, x, wq, wk, wv, wo_t, cols, block_avg, out):
    x_v = x.rearrange("b (k p) n -> b p k n", p=P)
    out_v = out.rearrange("b (k p) n -> b p k n", p=P)
    w_v = [w.rearrange("(k p) n -> p k n", p=P) for w in (wv, wo_t, wk, wq)]

    ctx = ExitStack()
    with ctx:
        def sb(name, shape, dt=FP32):
            return ctx.enter_context(nc.sbuf_tensor(name, shape, dt))

        def ps(name, shape):
            return ctx.enter_context(nc.psum_tensor(name, shape, FP32))

        def sem(name):
            return ctx.enter_context(nc.semaphore(name))

        xs = sb("xs", [P, 2, CT, N])
        h_hi, h_lo = (sb(f"h_{s}", [P, CT, N], FP32R) for s in ("hi", "lo"))
        t_hi, t_lo = (sb(f"t_{s}", [P, CT, N], FP32R) for s in ("hi", "lo"))
        v_hi, v_lo = (sb(f"v_{s}", [P, MT, C], FP32R) for s in ("hi", "lo"))
        p_hi, p_lo = (sb(f"p_{s}", [P, MT, HALF], FP32R) for s in ("hi", "lo"))
        g_hi, g_lo = (sb(f"g_{s}", [P, CT, C], FP32R) for s in ("hi", "lo"))
        u_hi, u_lo = (sb(f"u_{s}", [P, CT, C], FP32R) for s in ("hi", "lo"))
        stage = sb("stage", [P, MT + 1, HALF])
        colpart = sb("colpart", [P, HALF])
        colall = sb("colall", [P, HALF])
        inv = sb("inv", [P, HALF])
        scaled = sb("scaled", [P, 2, HALF])
        col = sb("col", [P, 6 * CT])
        avg = sb("avg", [P, P])
        ones = sb("ones", [P, P])
        stats = sb("stats", [P, CT, NB, 6])
        mv = sb("mv", [P, CT, 2])
        gmean, dmean, spread, veps, rstd, h_scale, shift, h_bias, minus_half = (
            sb(n, [P, CT]) for n in ("gmean", "dmean", "spread", "veps", "rstd", "h_scale", "shift", "h_bias",
                                     "minus_half"))
        keybias = sb("keybias", [P, MT])
        t_bias, k_dir, out_bias = (sb(n, [P, CT]) for n in ("t_bias", "k_dir", "out_bias"))
        bb, bb_sum, bqk = sb("bb", [P, CT]), sb("bb_sum", [P, 1]), sb("bqk", [P, 1])

        ring = ps("ring", [P, RING, HALF])
        av = ps("av", [P, CT, HALF])
        small = ps("small", [P, HALF])
        ps_keybias, ps_mean, ps_var = small[:, 0:MT], small[:, 8:8 + CT], small[:, 16:16 + CT]
        ps_tb, ps_kd, ps_ob, ps_bqk = small[:, 24:28], small[:, 32:36], small[:, 40:44], small[:, 48:49]

        raw_v = stage[:, 0:4, :].rearrange("p a n -> p (a n)").rearrange("p (k n) -> p k n", k=CT)
        raw_o = stage[:, 4:8, :].rearrange("p a n -> p (a n)").rearrange("p (k n) -> p k n", k=CT)
        raw_kq = xs[:, 1, :, :].rearrange("p k n -> p (k n)").rearrange("p (w k n) -> p w k n", w=2, k=CT)
        raw_k, raw_q = raw_kq[:, 0], raw_kq[:, 1]
        h_full = [stage[:, 2 * q:2 * q + 2, :].rearrange("p a n -> p (a n)") for q in range(2)]
        h_dot = stage[:, 4:6, :].rearrange("p a n -> p (a n)")

        s_col = sem("cols_loaded")
        s_wvo = [sem(f"wv_wo_loaded{k}") for k in range(CT)]
        s_wqk = sem("wq_wk_loaded")
        s_x = [sem(f"x_loaded{i}") for i in range(2)]
        s_stored = [sem(f"stored{i}") for i in range(2)]
        s_ones = sem("ones_set")
        s_half = sem("minus_half_set")
        s_prod = sem("weight_product_done")
        s_prod_hi = sem("weight_hi_done")
        s_prod_lo = sem("weight_lo_done")
        s_bb = sem("bias_dot_step")
        s_vec = sem("weight_vectors_done")
        s_vec_sb = sem("weight_vectors_copied")
        s_unit = sem("unit_done")
        s_kb = sem("keybias_summed")
        s_kbc = sem("keybias_copied")
        s_mean, s_var = sem("group_mean_done"), sem("group_var_done")
        s_pused = sem("p_tile_used")
        s_bank = sem("av_bank_done")
        s_thi, s_tlo = sem("t_hi_done"), sem("t_lo_done")
        s_vhi, s_vlo = sem("v_hi_done"), sem("v_lo_done")
        s_copied = sem("scores_copied")
        s_sub = sem("max_subtracted")
        s_exp = sem("exp_done")
        s_phi, s_plo = sem("p_hi_done"), sem("p_lo_done")
        s_maxh, s_maxp = sem("max_first_tiles"), sem("max_by_partition")
        s_sumh, s_sump = sem("sum_first_tiles"), sem("sum_by_partition")
        s_maxall, s_sumall = sem("max_all"), sem("sum_all")
        s_inv = sem("inverse_done")
        s_scaled, s_result = sem("output_scaled"), sem("result_done")
        s_stats, s_aggr = sem("stats_done"), sem("channel_stats_done")
        s_norm = sem("norm_step")
        s_rstd = sem("rstd_done")
        s_hf, s_hhi, s_hlo = sem("h_full_done"), sem("h_hi_done"), sem("h_lo_done")
        s_hdot = sem("h_dot_step")
        s_carrier = sem("wait_carrier")
        NORM = 8

        def lone_wait(eng, sem, count):
            eng.wait_ge(sem, count)
            eng.sem_inc(s_carrier, 1)

        block = ctx.enter_context(nc.Block())

        @block.sync
        def _(sp):
            sp.dma_start(col[:, :], cols).then_inc(s_col, DMA)
            sp.dma_start(avg[:, :], block_avg).then_inc(s_col, DMA)
            for k in range(CT):
                sp.dma_start(raw_v[:, k, :], w_v[0][:, k, :]).then_inc(s_wvo[k], DMA)
                sp.dma_start(raw_o[:, k, :], w_v[1][:, k, :]).then_inc(s_wvo[k], DMA)
            sp.dma_start(xs[:, 0, :, :], x_v[0]).then_inc(s_x[0], DMA)
            sp.dma_start(raw_k, w_v[2]).then_inc(s_wqk, DMA)
            sp.dma_start(raw_q, w_v[3]).then_inc(s_wqk, DMA)
            sp.wait_ge(s_prod, 2 * CT)
            sp.wait_ge(s_vec, 2)
            sp.dma_start(xs[:, 1, :, :], x_v[1]).then_inc(s_x[1], DMA)

            def image(b, par, load):
                for nb in range(NB):
                    sp.wait_ge(s_result, b * (2 * CT) + CT * (nb + 1))
                    sp.dma_start(out_v[b, :, :, nb * HALF:(nb + 1) * HALF],
                                 xs[:, par, :, nb * HALF:(nb + 1) * HALF]).then_inc(s_stored[par], DMA)
                if load:
                    sp.wait_ge(s_stored[par], (b - par) * DMA + 2 * DMA)
                    sp.dma_start(xs[:, par, :, :], x_v[b + 2]).then_inc(s_x[par], DMA)

            with sp.Fori(0, B - 3, 2) as b:
                image(b, 0, True)
                image(b + 1, 1, True)
            image(B - 2, 0, False)
            image(B - 1, 1, False)
            for par in range(2):
                sp.wait_ge(s_stored[par], B // 2 * 2 * DMA)

        @block.tensor
        def _(pe):
            def three(ps_out, a, w_hi, w_lo, m_hi, m_lo, first, last):
                nc.tensor.matmul(ps_out, w_hi, m_hi, start=first, stop=False)
                nc.tensor.matmul(ps_out, w_hi, m_lo, start=False, stop=False)
                return nc.tensor.matmul(ps_out, w_lo, m_hi, start=False, stop=last)

            def unit(j, pair, stat, mov):
                for k in range(CT):
                    ks, kc, ms, mc = stat(k) + mov(k)
                    a = three(ring[:, j % RING, :], pair, ks, kc, ms, mc, k == 0, k == CT - 1)
                a.then_inc(s_unit, 1)

            def weight_product(lhs, rhs, base, arrived):
                for k in range(CT):
                    arrived(k)
                    for i in range(CT):
                        if base and k == 0:
                            pe.wait_ge(s_prod_lo, i + 1)
                        a = nc.tensor.matmul(av[:, i, :], lhs[:, k, i * P:(i + 1) * P], rhs[:, k, :],
                                             start=k == 0, stop=k == CT - 1)
                        if k == CT - 1:
                            a.then_inc(s_prod, 1)

            def weight_vector(dst, w, bias):
                for i in range(CT):
                    for k in range(CT):
                        a = nc.tensor.matmul(dst[:, i:i + 1], w[:, k, i * P:(i + 1) * P],
                                             col[:, bias + k:bias + k + 1], start=k == 0, stop=k == CT - 1)
                return a

            def vo_arrived(k):
                pe.wait_ge(s_wvo[k], 2 * DMA)

            weight_product(raw_v, raw_o, 0, vo_arrived)
            pe.wait_ge(s_col, 2 * DMA)
            weight_vector(ps_ob, raw_o, BV).then_inc(s_vec, 1)
            pe.wait_ge(s_wqk, 2 * DMA)
            weight_product(raw_k, raw_q, 1, lambda k: None)
            pe.wait_ge(s_vec_sb, 1)
            weight_vector(ps_tb, raw_q, BK)
            weight_vector(ps_kd, raw_k, BQ)
            pe.wait_ge(s_ones, 1)
            pe.wait_ge(s_bb, 2)
            nc.tensor.matmul(ps_bqk, ones[:, :], bb_sum[:, :], start=True, stop=True).then_inc(s_vec, 1)

            def group_mean(n):
                pe.wait_ge(s_aggr, n * CT + CT)
                nc.tensor.matmul(ps_mean, avg[:, :], mv[:, :, 0], start=True, stop=True).then_inc(s_mean, 1)

            def group_var(n):
                pe.wait_ge(s_norm, n * NORM + 4)
                nc.tensor.matmul(ps_var, avg[:, :], spread[:, :], start=True, stop=True).then_inc(s_var, 1)

            pe.wait_ge(s_vec_sb, 4)
            group_mean(0)
            group_var(0)

            def output_half(b, nb, during=None):
                for m in range(MT):
                    if during and m == during[0]:
                        during[1]()
                    pe.wait_ge(s_plo, b * (2 * MT) + MT * nb + m + 1)
                    for c in range(CT):
                        if nb == 1 and m == 0:
                            pe.wait_ge(s_scaled, b * (2 * CT) + c + 1)
                        cs = slice(c * P, (c + 1) * P)
                        a = three(av[:, c, :], None, v_hi[:, m, cs], v_lo[:, m, cs], p_hi[:, m, :], p_lo[:, m, :],
                                  m == 0, m == MT - 1)
                        if m == MT - 1:
                            a.then_inc(s_bank, 1)
                    if nb == 0 and m < MT - 1:
                        a.then_inc(s_pused, 1)

            def image(b, more):
                pe.wait_ge(s_hlo, b * CT + CT)
                for j in range(NB * CT):
                    half, i = j // CT, j % CT
                    if j >= RING:
                        pe.wait_ge(s_tlo, b * 8 + j - RING + 1)
                    unit(T0 + j, None,
                         lambda k: (g_hi[:, k, i * P:(i + 1) * P], g_lo[:, k, i * P:(i + 1) * P]),
                         lambda k: (h_hi[:, k, half * HALF:(half + 1) * HALF],
                                    h_lo[:, k, half * HALF:(half + 1) * HALF]))
                    if j == RING:
                        pe.wait_ge(s_hdot, b * CT + CT)
                        for m in range(MT):
                            a = nc.tensor.matmul(ps_keybias[:, m:m + 1], h_dot[:, m * P:(m + 1) * P], ones[:, 0:1],
                                                 start=True, stop=True)
                        a.then_inc(s_kb, 1)

                def scores(nb):
                    for m in range(MT):
                        j = SCORES[nb] + m
                        if nb == 0 and m in (0, CT):
                            pe.wait_ge(s_tlo, b * 8 + m + CT)
                        if nb == 0 and m < RING:
                            pe.wait_ge(s_tlo, b * 8 + 8 - RING + m + 1)
                        elif nb == 1 and m < RING:
                            pe.wait_ge(s_vlo, b * 8 + 8 - RING + m + 1)
                        else:
                            pe.wait_ge(s_copied, b * (2 * MT) + MT * nb + m - RING + 1)
                        unit(j, None,
                             lambda k: (t_hi[:, k, m * P:(m + 1) * P], t_lo[:, k, m * P:(m + 1) * P]),
                             lambda k: (h_hi[:, k, nb * HALF:(nb + 1) * HALF],
                                        h_lo[:, k, nb * HALF:(nb + 1) * HALF]))

                scores(0)
                for m in range(MT):
                    if m < RING:
                        pe.wait_ge(s_copied, b * (2 * MT) + MT - RING + m + 1)
                    else:
                        pe.wait_ge(s_vlo, b * 8 + m - RING + 1)
                    unit(V0 + m, None,
                         lambda k: (h_hi[:, k, m * P:(m + 1) * P], h_lo[:, k, m * P:(m + 1) * P]),
                         lambda k: (u_hi[:, k, :], u_lo[:, k, :]))
                scores(1)
                if more:
                    group_mean(b + 1)
                pe.wait_ge(s_vlo, b * 8 + 8)
                output_half(b, 0, (3, lambda: group_var(b + 1)) if more else None)
                output_half(b, 1)

            with pe.Fori(0, B - 1) as b:
                image(b, True)
            image(B - 1, False)

        @block.scalar
        def _(act):
            def part_hi(out, ps_in, bias=0.0):
                return nc.scalar.activation(out, ps_in, ACT.Identity, bias=bias)

            for w in range(2):
                for i in range(CT):
                    act.wait_ge(s_prod, w * CT + i + 1)
                    part_hi((u_hi, g_hi)[w][:, i, :], av[:, i, :]).then_inc(s_prod_hi, 1)

            def normed(n, par, first):
                act.wait_ge(s_norm, n * NORM + NORM)
                for k in range(CT):
                    if k == 0:
                        if first:
                            act.wait_ge(s_prod, CT)
                            act.wait_ge(s_vec, 1)
                        else:
                            act.wait_ge(s_sumh, n * 2)
                            act.wait_ge(s_plo, n * (2 * MT) - MT // 2)
                    elif k >= 2:
                        act.wait_ge(s_hlo, n * CT + k - 1)
                        act.wait_ge(s_hdot, n * CT + k - 1)
                    nc.scalar.activation(h_full[k % 2], xs[:, par, k, :], ACT.Identity, bias=h_bias[:, k:k + 1],
                                         scale=h_scale[:, k:k + 1]).then_inc(s_hf, 1)
                    nc.scalar.activation(h_hi[:, k, :], xs[:, par, k, :], ACT.Identity, bias=h_bias[:, k:k + 1],
                                         scale=h_scale[:, k:k + 1]).then_inc(s_hhi, 1)

            normed(0, 0, True)
            act.wait_ge(s_vec_sb, 4)

            def copy_scores(b, nb):
                for m in range(MT):
                    act.wait_ge(s_unit, b * UNITS + SCORES[nb] + m + 1)
                    if nb == 1 and m in (0, MT // 2):
                        act.wait_ge(s_plo, b * (2 * MT) + m + MT // 2)
                        act.wait_ge(s_sumh if m == 0 else s_sump, b * 2 + 1)
                    nc.scalar.activation(stage[:, m, :], ring[:, (SCORES[nb] + m) % RING, :], ACT.Identity,
                                         bias=keybias[:, m:m + 1]).then_inc(s_copied, 1)

            def exponential(b, nb, m):
                act.wait_ge(s_sub, b * (2 * MT) + MT * nb + m + 1)
                nc.scalar.activation(stage[:, m, :], stage[:, m, :], ACT.Exp, scale=SCALE).then_inc(s_exp, 1)

            def p_part(b, nb, m):
                act.wait_ge(s_exp, b * (2 * MT) + MT * nb + m + 1)
                if nb == 1:
                    if m < MT - 1:
                        act.wait_ge(s_pused, b * (MT - 1) + m + 1)
                    else:
                        act.wait_ge(s_bank, b * (2 * CT) + CT)
                nc.scalar.activation(p_hi[:, m, :], stage[:, m, :], ACT.Copy).then_inc(s_phi, 1)

            def v_part(b, m):
                act.wait_ge(s_unit, b * UNITS + V0 + m + 1)
                part_hi(v_hi[:, m, :], ring[:, (V0 + m) % RING, :]).then_inc(s_vhi, 1)

            def image(b, par, more):
                for j in range(NB * CT):
                    half, i = j // CT, j % CT
                    act.wait_ge(s_unit, b * UNITS + T0 + j + 1)
                    part_hi(t_hi[:, i, half * HALF:(half + 1) * HALF], ring[:, (T0 + j) % RING, :],
                            t_bias[:, i:i + 1]).then_inc(s_thi, 1)
                act.wait_ge(s_kb, b + 1)
                nc.scalar.activation(keybias[:, :], ps_keybias, ACT.Identity, bias=bqk[:, :]).then_inc(s_kbc, 1)
                act.wait_ge(s_kbc, b + 1)
                copy_scores(b, 0)
                for m in range(2):
                    v_part(b, m)
                for m in range(MT):
                    exponential(b, 0, m)
                    if m + 2 < MT:
                        v_part(b, m + 2)
                    p_part(b, 0, m)
                copy_scores(b, 1)
                exponential(b, 1, 0)
                for m in range(MT):
                    if m + 1 < MT:
                        exponential(b, 1, m + 1)
                    p_part(b, 1, m)
                if more:
                    normed(b + 1, 1 - par, False)

            with act.Fori(0, B - 3, 2) as b:
                image(b, 0, True)
                image(b + 1, 1, True)
            image(B - 2, 0, True)
            image(B - 1, 1, False)

        @block.gpsimd
        def _(pool):
            nc.gpsimd.memset(minus_half[:, :], -0.5).then_inc(s_half, 1)
            pool.wait_ge(s_half, 1)

            def inverse_deviation(n):
                pool.wait_ge(s_norm, n * NORM + 5)
                nc.gpsimd.tensor_tensor(rstd[:, :], veps[:, :], minus_half[:, :], ALU.pow).then_inc(s_rstd, 1)

            def h_part(n, k):
                pool.wait_ge(s_hf, n * CT + k + 1)
                pool.wait_ge(s_hhi, n * CT + k + 1)
                nc.gpsimd.tensor_tensor(h_lo[:, k, :], h_full[k % 2], h_hi[:, k, :].bitcast(FP32),
                                        ALU.subtract).then_inc(s_hlo, 1)

            def over_partitions(b, nb, op, ready, done):
                lone_wait(pool, ready, b * 2 + nb + 1)
                nc.gpsimd.partition_all_reduce(colall[:, :], colpart[:, :], P, op).then_inc(done, 1)

            inverse_deviation(0)
            for k in range(CT):
                h_part(0, k)

            def image(b, more):
                over_partitions(b, 0, bass.bass_isa.ReduceOp.max, s_maxp, s_maxall)
                over_partitions(b, 0, bass.bass_isa.ReduceOp.add, s_sump, s_sumall)
                over_partitions(b, 1, bass.bass_isa.ReduceOp.max, s_maxp, s_maxall)
                if more:
                    inverse_deviation(b + 1)
                over_partitions(b, 1, bass.bass_isa.ReduceOp.add, s_sump, s_sumall)
                if more:
                    for k in range(CT):
                        h_part(b + 1, k)

            with pool.Fori(0, B - 1) as b:
                image(b, True)
            image(B - 1, False)

        @block.vector
        def _(dve):
            nc.vector.memset(ones[:, :], 1.0).then_inc(s_ones, 1)
            dve.wait_ge(s_col, 2 * DMA)
            nc.vector.tensor_tensor(bb[:, :], col[:, BQ:BQ + CT], col[:, BK:BK + CT], ALU.mult).then_inc(s_bb, 1)
            dve.wait_ge(s_bb, 1)
            nc.vector.tensor_reduce(bb_sum[:, :], bb[:, :], AX.X, ALU.add).then_inc(s_bb, 1)

            def weight_lo(w, i):
                dve.wait_ge(s_prod_hi, w * CT + i + 1)
                hi, lo = ((u_hi, u_lo), (g_hi, g_lo))[w]
                nc.vector.tensor_tensor(lo[:, i, :], av[:, i, :], hi[:, i, :].bitcast(FP32),
                                        ALU.subtract).then_inc(s_prod_lo, 1)

            def channel_stats(n, par, loaded):
                dve.wait_ge(s_x[par], loaded)
                for k in range(CT):
                    for s in range(NB):
                        nc.vector.bn_stats(stats[:, k, s, :],
                                           xs[:, par, k, s * HALF:(s + 1) * HALF]).then_inc(s_stats, 1)
                lone_wait(dve, s_stats, (n + 1) * (CT * NB))
                for k in range(CT):
                    nc.vector.bn_aggr(mv[:, k, :], stats[:, k, :, :].rearrange("p s e -> p (s e)")).then_inc(s_aggr, 1)

            def about_mean(n):
                at = n * NORM
                dve.wait_ge(s_mean, n + 1)
                nc.vector.tensor_copy(gmean[:, :], ps_mean).then_inc(s_norm, 1)
                nc.vector.tensor_tensor(dmean[:, :], ps_mean, mv[:, :, 0], ALU.subtract).then_inc(s_norm, 1)
                dve.wait_ge(s_norm, at + 2)
                nc.vector.tensor_tensor(shift[:, :], dmean[:, :], dmean[:, :], ALU.mult).then_inc(s_norm, 1)
                dve.wait_ge(s_norm, at + 3)
                nc.vector.tensor_tensor(spread[:, :], shift[:, :], mv[:, :, 1], ALU.add).then_inc(s_norm, 1)

            def variance(n):
                dve.wait_ge(s_var, n + 1)
                nc.vector.tensor_scalar(veps[:, :], ps_var, EPS, None, ALU.add).then_inc(s_norm, 1)

            def affine(n):
                at = n * NORM
                dve.wait_ge(s_rstd, n + 1)
                nc.vector.tensor_tensor(h_scale[:, :], rstd[:, :], col[:, GW:GW + CT], ALU.mult).then_inc(s_norm, 1)
                dve.wait_ge(s_norm, at + 6)
                nc.vector.tensor_tensor(shift[:, :], h_scale[:, :], gmean[:, :], ALU.mult).then_inc(s_norm, 1)
                dve.wait_ge(s_norm, at + 7)
                nc.vector.tensor_tensor(h_bias[:, :], col[:, GB:GB + CT], shift[:, :], ALU.subtract).then_inc(s_norm, 1)

            def dot_step(n, k):
                dve.wait_ge(s_hf, n * CT + k + 1)
                if k == 0:
                    nc.vector.tensor_scalar(h_dot, h_full[0], k_dir[:, 0:1], None, ALU.mult).then_inc(s_hdot, 1)
                else:
                    dve.wait_ge(s_hdot, n * CT + k)
                    nc.vector.scalar_tensor_tensor(h_dot, h_full[k % 2], k_dir[:, k:k + 1], h_dot, ALU.mult,
                                                   ALU.add).then_inc(s_hdot, 1)

            for i in range(CT):
                weight_lo(0, i)
            channel_stats(0, 0, DMA)
            dve.wait_ge(s_vec, 1)
            nc.vector.tensor_tensor(out_bias[:, :], ps_ob, col[:, BO:BO + CT], ALU.add).then_inc(s_vec_sb, 1)
            for i in range(CT):
                weight_lo(1, i)
            dve.wait_ge(s_vec, 2)
            nc.vector.tensor_copy(t_bias[:, :], ps_tb).then_inc(s_vec_sb, 1)
            nc.vector.tensor_copy(k_dir[:, :], ps_kd).then_inc(s_vec_sb, 1)
            nc.vector.tensor_copy(bqk[:, :], ps_bqk).then_inc(s_vec_sb, 1)
            about_mean(0)
            variance(0)
            affine(0)
            dve.wait_ge(s_vec_sb, 4)
            for k in range(CT):
                dot_step(0, k)

            def over_tiles(b, nb, first, op, ready, half_done, done):
                if first:
                    dve.wait_ge(ready, b * (2 * MT) + MT * nb + MT // 2)
                    nc.vector.tensor_reduce(stage[:, MT, :], stage[:, 0:MT // 2, :].rearrange("p s n -> p n s"),
                                            AX.X, op).then_inc(half_done, 1)
                else:
                    dve.wait_ge(ready, b * (2 * MT) + MT * (nb + 1))
                    dve.wait_ge(half_done, b * 2 + nb + 1)
                    nc.vector.tensor_reduce(colpart[:, :], stage[:, MT // 2:MT + 1, :].rearrange("p s n -> p n s"),
                                            AX.X, op).then_inc(done, 1)

            def key_max(b, nb, first):
                over_tiles(b, nb, first, ALU.max, s_copied, s_maxh, s_maxp)

            def key_sum(b, nb, first):
                over_tiles(b, nb, first, ALU.add, s_exp, s_sumh, s_sump)

            def subtract_max(b, nb, m):
                if m == 0:
                    dve.wait_ge(s_maxall, b * 2 + nb + 1)
                nc.vector.tensor_tensor(stage[:, m, :], stage[:, m, :], colall[:, :], ALU.subtract).then_inc(s_sub, 1)

            def p_rest(b, nb, m):
                dve.wait_ge(s_phi, b * (2 * MT) + MT * nb + m + 1)
                nc.vector.tensor_tensor(p_lo[:, m, :], stage[:, m, :], p_hi[:, m, :].bitcast(FP32),
                                        ALU.subtract).then_inc(s_plo, 1)

            def v_rest(b, m):
                dve.wait_ge(s_vhi, b * 8 + m + 1)
                nc.vector.tensor_tensor(v_lo[:, m, :], ring[:, (V0 + m) % RING, :], v_hi[:, m, :].bitcast(FP32),
                                        ALU.subtract).then_inc(s_vlo, 1)

            def inverse(b, nb):
                dve.wait_ge(s_sumall, b * 2 + nb + 1)
                nc.vector.reciprocal(inv[:, :], colall[:, :]).then_inc(s_inv, 1)

            def scale_output(b, nb, c):
                dve.wait_ge(s_inv, b * 2 + nb + 1)
                dve.wait_ge(s_bank, b * (2 * CT) + CT * nb + c + 1)
                if c >= 2:
                    dve.wait_ge(s_result, b * (2 * CT) + CT * nb + c - 1)
                nc.vector.tensor_tensor(scaled[:, c % 2, :], av[:, c, :], inv[:, :], ALU.mult).then_inc(s_scaled, 1)

            def add_input(b, par, nb, c):
                dve.wait_ge(s_scaled, b * (2 * CT) + CT * nb + c + 1)
                here = xs[:, par, c, nb * HALF:(nb + 1) * HALF]
                nc.vector.scalar_tensor_tensor(here, scaled[:, c % 2, :], out_bias[:, c:c + 1], here, ALU.add,
                                               ALU.add).then_inc(s_result, 1)

            def results(b, par, nb):
                scale_output(b, nb, 0)
                scale_output(b, nb, 1)
                for c in range(2, CT + 2):
                    add_input(b, par, nb, c - 2)
                    if c < CT:
                        scale_output(b, nb, c)

            def image(b, par, more):
                for j in range(NB * CT):
                    half, i = j // CT, j % CT
                    here = slice(half * HALF, (half + 1) * HALF)
                    dve.wait_ge(s_thi, b * 8 + j + 1)
                    nc.vector.scalar_tensor_tensor(t_lo[:, i, here], ring[:, (T0 + j) % RING, :], t_bias[:, i:i + 1],
                                                   t_hi[:, i, here].bitcast(FP32), ALU.add,
                                                   ALU.subtract).then_inc(s_tlo, 1)
                key_max(b, 0, True)
                key_max(b, 0, False)
                for m in range(2):
                    v_rest(b, m)
                for m in range(MT):
                    subtract_max(b, 0, m)
                    if m >= 1:
                        p_rest(b, 0, m - 1)
                    if m + 2 < MT:
                        v_rest(b, m + 2)
                    if m == MT // 2 + 1:
                        key_sum(b, 0, True)
                p_rest(b, 0, MT - 1)
                key_sum(b, 0, False)
                dve.wait_ge(s_sump, b * 2 + 1)
                key_max(b, 1, True)
                inverse(b, 0)
                if more:
                    channel_stats(b + 1, 1 - par, (b - par) * (DMA // 2) + DMA * (1 + par))
                key_max(b, 1, False)
                if more:
                    about_mean(b + 1)
                subtract_max(b, 1, 0)
                subtract_max(b, 1, 1)
                for m in range(2, MT):
                    subtract_max(b, 1, m)
                    p_rest(b, 1, m - 2)
                    if more and m == 4:
                        variance(b + 1)
                    if more and m == 6:
                        affine(b + 1)
                    if m == MT // 2 + 1:
                        key_sum(b, 1, True)
                p_rest(b, 1, MT - 2)
                results(b, par, 0)
                p_rest(b, 1, MT - 1)
                key_sum(b, 1, False)
                if more:
                    dve.wait_ge(s_sump, b * 2 + 2)
                    for k in range(CT):
                        dot_step(b + 1, k)
                inverse(b, 1)
                results(b, par, 1)

            with dve.Fori(0, B - 3, 2) as b:
                image(b, 0, True)
                image(b + 1, 1, True)
            image(B - 2, 0, True)
            image(B - 1, 1, False)


def kernel(x, L0_conv_gn_w, L0_conv_gn_b, L0_conv_qkv_w, L0_conv_qkv_b, L0_conv_out_w, L0_conv_out_b):
    import concourse.bacc as bacc
    from concourse.bass_utils import run_bass_kernel_spmd

    rows = np.concatenate([np.asarray(a).reshape(-1, P) for a in
                           (L0_conv_qkv_b, L0_conv_gn_w, L0_conv_gn_b, L0_conv_out_b)])
    arrays = {
        "x_in": np.ascontiguousarray(x).reshape(B, C, N),
        "wq": np.ascontiguousarray(L0_conv_qkv_w[0:C]),
        "wk": np.ascontiguousarray(L0_conv_qkv_w[C:2 * C]),
        "wv": np.ascontiguousarray(L0_conv_qkv_w[2 * C:3 * C]),
        "wo_t": np.ascontiguousarray(np.asarray(L0_conv_out_w).T),
        "cols": np.ascontiguousarray(rows.T),
        "block_avg": np.kron(np.eye(P * GROUPS // C), np.full((C // GROUPS,) * 2, GROUPS / C)).astype(np.float32),
    }
    nc = bacc.Bacc("TRN2", target_bir_lowering=False, num_devices=1, dynamic_dma_scratch_size=1024)
    ins = [nc.dram_tensor(n, a.shape, mybir.dt.from_np(a.dtype), kind="ExternalInput").ap() for n, a in arrays.items()]
    out = nc.dram_tensor("out", (B, C, N), FP32, kind="ExternalOutput").ap()
    attention_kernel(nc, *ins, out)
    r = run_bass_kernel_spmd(nc, [arrays], core_ids=[0])
    return r.results[0]["out"].reshape(B, C, H, W)
```

```python
from contextlib import ExitStack

import numpy as np

import concourse.bass as bass
from concourse import mybir


FP32 = mybir.dt.float32
FP32R = mybir.dt.float32r
BF16 = mybir.dt.bfloat16
ALU = mybir.AluOpType
ACT = mybir.ActivationFunctionType
AX = mybir.AxisListType

P = 128
B, C, H, W = 16, 512, 32, 32
N = H * W
GROUPS = 32
EPS = 1e-5
SCALE = 1.0 / float(C) ** 0.5
CT = C // P
MT = N // P
HALF = 512
NB = N // HALF
RING = 3
UNITS = NB * CT + MT + NB * MT
DMA = 16

T0 = 0
S0 = T0 + NB * CT
V0 = S0 + MT
S1 = V0 + MT
SCORES = (S0, S1)
BQ, BK, BV, GW, GB, BO = (CT * i for i in range(6))


def attention_kernel(nc, x, wq, wk, wv, wo_t, cols, block_avg, out):
    x_v = x.rearrange("b (k p) n -> b p k n", p=P)
    out_v = out.rearrange("b (k p) n -> b p k n", p=P)
    w_v = [[w.rearrange("(k p) n -> p k n", p=P) for w in pair] for pair in ((wk, wq), (wv, wo_t))]

    ctx = ExitStack()
    with ctx:
        def sb(name, shape, dt=FP32):
            return ctx.enter_context(nc.sbuf_tensor(name, shape, dt))

        def ps(name, shape):
            return ctx.enter_context(nc.psum_tensor(name, shape, FP32))

        def sem(name):
            return ctx.enter_context(nc.semaphore(name))

        xs = sb("xs", [P, 2, CT, N])
        h_hi, h_lo = (sb(f"h_{s}", [P, CT, N], FP32R) for s in ("hi", "lo"))
        t_hi, t_lo = (sb(f"t_{s}", [P, CT, N], FP32R) for s in ("hi", "lo"))
        v_hi, v_lo = (sb(f"v_{s}", [P, MT, C], FP32R) for s in ("hi", "lo"))
        p_hi, p_lo = (sb(f"p_{s}", [P, MT, HALF], FP32R) for s in ("hi", "lo"))
        g_hi, g_lo = (sb(f"g_{s}", [P, CT, C], FP32R) for s in ("hi", "lo"))
        u_hi, u_lo = (sb(f"u_{s}", [P, CT, C], FP32R) for s in ("hi", "lo"))
        stage = sb("stage", [P, MT + 1, HALF])
        colpart = sb("colpart", [P, HALF])
        colall = sb("colall", [P, HALF])
        inv = sb("inv", [P, HALF])
        scaled = sb("scaled", [P, 2, HALF])
        col = sb("col", [P, 6 * CT])
        avg = sb("avg", [P, P])
        ones, ones_bf = sb("ones", [P, 1]), sb("ones_bf", [P, 1], BF16)
        stats = sb("stats", [P, CT, NB, 6])
        mv = sb("mv", [P, CT, 2])
        gmean, dmean, spread, veps, rstd, h_scale, shift, h_bias, minus_half = (
            sb(n, [P, CT]) for n in ("gmean", "dmean", "spread", "veps", "rstd", "h_scale", "shift", "h_bias",
                                     "minus_half"))
        keybias = sb("keybias", [P, MT])
        t_bias, k_dir, out_bias = (sb(n, [P, CT]) for n in ("t_bias", "k_dir", "out_bias"))
        bb, bb_sum, bqk = sb("bb", [P, CT]), sb("bb_sum", [P, 1]), sb("bqk", [P, 1])

        ring = ps("ring", [P, RING, HALF])
        av = ps("av", [P, CT, HALF])
        small = ps("small", [P, HALF])
        ps_keybias = small[:, 0:MT]
        ps_mean, ps_var, ps_kd, ps_tb, ps_ob = (small[:, c:c + CT] for c in (16, 24, 32, 40, 48))

        raw = xs[:, 1, :, :].rearrange("p k n -> p (k n)").rearrange("p (k w n) -> p k w n", k=CT, w=2)
        w_hi, w_lo = (p_hi, v_hi), (p_lo, v_lo)
        product_hi, product_lo = (g_hi, u_hi), (g_lo, u_lo)
        product_bank = ([ring[:, 0, :], ring[:, 1, :], ring[:, 2, :], av[:, 0, :]],
                        [av[:, 1, :], av[:, 2, :], av[:, 3, :], ring[:, 0, :]])
        h_full = [stage[:, 2 * q:2 * q + 2, :].rearrange("p a n -> p (a n)") for q in range(2)]
        h_dot = stage[:, 4:6, :].rearrange("p a n -> p (a n)")
        dot_part = [stage[:, 6 + i, :].bitcast(BF16) for i in range(3)]
        weighted = [scaled[:, 0, :], scaled[:, 1, :], inv[:, :]]
        scaled_at = [scaled[:, 0, :], scaled[:, 1, :], colpart[:, :]]

        s_col = sem("cols_loaded")
        s_w = [[sem(f"weights{w}_loaded{k}") for k in range(CT)] for w in range(2)]
        s_first = [sem(f"first_image_loaded{k}") for k in range(CT)]
        s_x = [sem(f"x_loaded{i}") for i in range(2)]
        s_stored = [sem(f"stored{i}") for i in range(2)]
        s_ones = sem("ones_set")
        s_half = sem("minus_half_set")
        s_whi = sem("weights_hi_done")
        s_wlo = [sem(f"weights{w}_lo_done") for w in range(2)]
        s_weighted = [sem(f"rows_weighted{v}") for v in range(3)]
        s_prod = sem("weight_product_done")
        s_prod_hi, s_prod_lo = sem("product_hi_done"), sem("product_lo_done")
        s_bb, s_bqk = sem("bias_dot_step"), sem("bias_dot_done")
        s_vec = sem("weight_vector_done")
        s_vec_sb = sem("weight_vectors_copied")
        s_unit = sem("unit_done")
        s_kb = sem("keybias_summed")
        s_kbc = sem("keybias_copied")
        s_mean, s_var = sem("group_mean_done"), sem("group_var_done")
        s_pused = sem("p_tile_used")
        s_bank = sem("av_bank_done")
        s_thi, s_tlo = sem("t_hi_done"), sem("t_lo_done")
        s_vhi, s_vlo = sem("v_hi_done"), sem("v_lo_done")
        s_copied = sem("scores_copied")
        s_sub = sem("max_subtracted")
        s_exp = sem("exp_done")
        s_phi, s_plo = sem("p_hi_done"), sem("p_lo_done")
        s_maxh, s_maxp = sem("max_first_tiles"), sem("max_by_partition")
        s_sumh, s_sump = sem("sum_first_tiles"), sem("sum_by_partition")
        s_maxall, s_sumall = sem("max_all"), sem("sum_all")
        s_inv = sem("inverse_done")
        s_scaled, s_result = sem("output_scaled"), sem("result_done")
        s_stats, s_aggr = sem("stats_done"), sem("channel_stats_done")
        s_norm = sem("norm_step")
        s_rstd = sem("rstd_done")
        s_hf, s_hhi, s_hlo = sem("h_full_done"), sem("h_hi_done"), sem("h_lo_done")
        s_hdot = sem("h_dot_step")
        s_dpart = [sem(f"dot_part{i}_done") for i in range(3)]
        s_drest = sem("dot_rest_done")
        s_carrier = sem("wait_carrier")
        NORM = 8

        def lone_wait(eng, sem, count):
            eng.wait_ge(sem, count)
            eng.sem_inc(s_carrier, 1)

        block = ctx.enter_context(nc.Block())

        @block.sync
        def _(sp):
            def load_weights(w, k):
                for i in range(2):
                    sp.dma_start(raw[:, k, i, :], w_v[w][i][:, k, :]).then_inc(s_w[w][k], DMA)

            load_weights(0, 0)
            sp.dma_start(col[:, :], cols).then_inc(s_col, DMA)
            sp.dma_start(avg[:, :], block_avg).then_inc(s_col, DMA)
            for k in range(1, CT):
                load_weights(0, k)
            for k in range(CT):
                sp.dma_start(xs[:, 0, k, :], x_v[0, :, k, :]).then_inc(s_first[k], DMA)
            for k in range(CT):
                sp.wait_ge(s_wlo[0], k + 1)
                sp.wait_ge(s_weighted[0], k + 1)
                sp.wait_ge(s_weighted[1], k + 1)
                load_weights(1, k)
            sp.wait_ge(s_wlo[1], CT)
            sp.wait_ge(s_weighted[2], CT)
            sp.dma_start(xs[:, 1, :, :], x_v[1]).then_inc(s_x[1], DMA)

            def image(b, par, load, last=False):
                for nb in range(NB):
                    if last and nb == NB - 1:
                        for c in range(CT):
                            sp.wait_ge(s_result, b * (2 * CT) + CT * nb + c + 1)
                            sp.dma_start(out_v[b, :, c, nb * HALF:(nb + 1) * HALF],
                                         xs[:, par, c, nb * HALF:(nb + 1) * HALF]).then_inc(s_stored[par], DMA)
                        continue
                    sp.wait_ge(s_result, b * (2 * CT) + CT * (nb + 1))
                    sp.dma_start(out_v[b, :, :, nb * HALF:(nb + 1) * HALF],
                                 xs[:, par, :, nb * HALF:(nb + 1) * HALF]).then_inc(s_stored[par], DMA)
                if load:
                    sp.wait_ge(s_stored[par], (b - par) * DMA + 2 * DMA)
                    sp.dma_start(xs[:, par, :, :], x_v[b + 2]).then_inc(s_x[par], DMA)

            with sp.Fori(0, B - 3, 2) as b:
                image(b, 0, True)
                image(b + 1, 1, True)
            image(B - 2, 0, False)
            image(B - 1, 1, False, last=True)
            sp.wait_ge(s_stored[0], B // 2 * 2 * DMA)
            sp.wait_ge(s_stored[1], (B // 2 * 2 - 1 + CT) * DMA)

        @block.tensor
        def _(pe):
            def three(ps_out, st_hi, st_lo, m_hi, m_lo, first, last):
                nc.tensor.matmul(ps_out, st_hi, m_hi, start=first, stop=False)
                nc.tensor.matmul(ps_out, st_hi, m_lo, start=False, stop=False)
                return nc.tensor.matmul(ps_out, st_lo, m_hi, start=False, stop=last)

            def unit(j, stat, mov):
                for k in range(CT):
                    a = three(ring[:, j % RING, :], *stat(k), *mov(k), k == 0, k == CT - 1)
                a.then_inc(s_unit, 1)

            def weight_product(w, k):
                pe.wait_ge(s_wlo[w], k + 1)
                for i in range(CT):
                    if w and k == 0 and i == CT - 1:
                        pe.wait_ge(s_prod_lo, 1)
                    cs = slice(i * P, (i + 1) * P)
                    a = three(product_bank[w][i], w_hi[w][:, 2 * k, cs], w_lo[w][:, 2 * k, cs],
                              w_hi[w][:, 2 * k + 1, :], w_lo[w][:, 2 * k + 1, :], k == 0, k == CT - 1)
                    if k == CT - 1:
                        a.then_inc(s_prod, 1)

            def weight_vector(v, dst):
                pe.wait_ge(s_weighted[v], CT)
                for i in range(CT):
                    a = nc.tensor.matmul(dst[:, i:i + 1], weighted[v][:, i * P:(i + 1) * P], ones[:, :],
                                         start=True, stop=True)
                a.then_inc(s_vec, 1)

            def group_mean(n):
                pe.wait_ge(s_aggr, n * CT + CT)
                nc.tensor.matmul(ps_mean, avg[:, :], mv[:, :, 0], start=True, stop=True).then_inc(s_mean, 1)

            def group_var(n):
                pe.wait_ge(s_norm, n * NORM + 4)
                nc.tensor.matmul(ps_var, avg[:, :], spread[:, :], start=True, stop=True).then_inc(s_var, 1)

            for k in range(CT):
                weight_product(0, k)
            pe.wait_ge(s_ones, 2)
            weight_vector(0, ps_kd)
            weight_vector(1, ps_tb)
            weight_product(1, 0)
            pe.wait_ge(s_vec_sb, 2)
            pe.wait_ge(s_col, 2 * DMA)
            group_mean(0)
            weight_product(1, 1)
            group_var(0)
            weight_product(1, 2)
            weight_product(1, 3)
            pe.wait_ge(s_norm, 5)
            weight_vector(2, ps_ob)
            pe.wait_ge(s_vec_sb, 3)
            pe.wait_ge(s_prod_lo, CT + 1)

            def output_half(b, nb, during={}):
                for m in range(MT):
                    if m in during:
                        during[m]()
                    pe.wait_ge(s_plo, b * (2 * MT) + MT * nb + m + 1)
                    for c in range(CT):
                        if nb == 1 and m == 0:
                            pe.wait_ge(s_scaled, b * (2 * CT) + c + 1)
                        cs = slice(c * P, (c + 1) * P)
                        a = three(av[:, c, :], v_hi[:, m, cs], v_lo[:, m, cs], p_hi[:, m, :], p_lo[:, m, :],
                                  m == 0, m == MT - 1)
                        if m == MT - 1:
                            a.then_inc(s_bank, 1)
                    if nb == 0 and m < MT - 1:
                        a.then_inc(s_pused, 1)

            def image(b, more):
                pe.wait_ge(s_hlo, b * CT + CT)
                for j in range(NB * CT):
                    half, i = j // CT, j % CT
                    if j >= RING:
                        pe.wait_ge(s_tlo, b * 8 + j - RING + 1)
                    unit(T0 + j,
                         lambda k: (g_hi[:, k, i * P:(i + 1) * P], g_lo[:, k, i * P:(i + 1) * P]),
                         lambda k: (h_hi[:, k, half * HALF:(half + 1) * HALF],
                                    h_lo[:, k, half * HALF:(half + 1) * HALF]))
                    if j == CT + 1:
                        for part in range(3):
                            pe.wait_ge(s_dpart[part], b + 1)
                        for m in range(MT):
                            for part in range(3):
                                a = nc.tensor.matmul(ps_keybias[:, m:m + 1], dot_part[part][:, m * P:(m + 1) * P],
                                                     ones_bf[:, :], start=part == 0, stop=part == 2)
                        a.then_inc(s_kb, 1)

                def scores(nb):
                    for m in range(MT):
                        j = SCORES[nb] + m
                        if nb == 0 and m in (0, CT):
                            pe.wait_ge(s_tlo, b * 8 + m + CT)
                        if nb == 0 and m < RING:
                            pe.wait_ge(s_tlo, b * 8 + 8 - RING + m + 1)
                        elif nb == 1 and m < RING:
                            pe.wait_ge(s_vlo, b * 8 + 8 - RING + m + 1)
                        else:
                            pe.wait_ge(s_copied, b * (2 * MT) + MT * nb + m - RING + 1)
                        unit(j,
                             lambda k: (t_hi[:, k, m * P:(m + 1) * P], t_lo[:, k, m * P:(m + 1) * P]),
                             lambda k: (h_hi[:, k, nb * HALF:(nb + 1) * HALF],
                                        h_lo[:, k, nb * HALF:(nb + 1) * HALF]))

                scores(0)
                pe.wait_ge(s_prod_lo, 2 * CT)
                for m in range(MT):
                    if m < RING:
                        pe.wait_ge(s_copied, b * (2 * MT) + MT - RING + m + 1)
                    else:
                        pe.wait_ge(s_vlo, b * 8 + m - RING + 1)
                    unit(V0 + m,
                         lambda k: (h_hi[:, k, m * P:(m + 1) * P], h_lo[:, k, m * P:(m + 1) * P]),
                         lambda k: (u_hi[:, k, :], u_lo[:, k, :]))
                scores(1)
                pe.wait_ge(s_vlo, b * 8 + 8)
                output_half(b, 0, {2: lambda: group_mean(b + 1), 4: lambda: group_var(b + 1)} if more else {})
                output_half(b, 1)

            with pe.Fori(0, B - 1) as b:
                image(b, True)
            image(B - 1, False)

        @block.scalar
        def _(act):
            def part_hi(out, ps_in, bias=0.0):
                return nc.scalar.activation(out, ps_in, ACT.Identity, bias=bias)

            def weight_part(w, k):
                act.wait_ge(s_w[w][k], 2 * DMA)
                nc.scalar.activation(w_hi[w][:, 2 * k:2 * k + 2, :], raw[:, k, :, :], ACT.Copy).then_inc(s_whi, 1)

            def product_part(w, i):
                act.wait_ge(s_prod, w * CT + i + 1)
                part_hi(product_hi[w][:, i, :], product_bank[w][i]).then_inc(s_prod_hi, 1)

            def normed(n, par, k, first=False):
                if k == 0:
                    act.wait_ge(s_norm, n * NORM + NORM)
                    if not first:
                        act.wait_ge(s_sumh, n * 2)
                        act.wait_ge(s_plo, n * (2 * MT) - MT // 2)
                elif k >= 2:
                    act.wait_ge(s_hlo, n * CT + k - 1)
                    act.wait_ge(s_hdot, n * CT + k - 1)
                for out, done in ((h_full[k % 2], s_hf), (h_hi[:, k, :], s_hhi)):
                    nc.scalar.activation(out, xs[:, par, k, :], ACT.Identity, bias=h_bias[:, k:k + 1],
                                         scale=h_scale[:, k:k + 1]).then_inc(done, 1)

            for k in range(CT):
                weight_part(0, k)
            weight_part(1, 0)
            weight_part(1, 1)
            for i in range(CT):
                product_part(0, i)
            weight_part(1, 2)
            weight_part(1, 3)
            for k in range(CT):
                normed(0, 0, k, True)
            product_part(1, 3)
            for i in range(CT - 1):
                product_part(1, i)
            act.wait_ge(s_vec_sb, 2)
            act.wait_ge(s_bqk, 1)

            def copy_scores(b, nb):
                for m in range(MT):
                    act.wait_ge(s_unit, b * UNITS + SCORES[nb] + m + 1)
                    if nb == 1 and m in (0, MT // 2):
                        act.wait_ge(s_plo, b * (2 * MT) + m + MT // 2)
                        act.wait_ge(s_sumh if m == 0 else s_sump, b * 2 + 1)
                    nc.scalar.activation(stage[:, m, :], ring[:, (SCORES[nb] + m) % RING, :], ACT.Identity,
                                         bias=keybias[:, m:m + 1]).then_inc(s_copied, 1)

            def exponential(b, nb, m):
                act.wait_ge(s_sub, b * (2 * MT) + MT * nb + m + 1)
                nc.scalar.activation(stage[:, m, :], stage[:, m, :], ACT.Exp, scale=SCALE).then_inc(s_exp, 1)

            def p_part(b, nb, m):
                act.wait_ge(s_exp, b * (2 * MT) + MT * nb + m + 1)
                if nb == 1:
                    if m < MT - 1:
                        act.wait_ge(s_pused, b * (MT - 1) + m + 1)
                    else:
                        act.wait_ge(s_bank, b * (2 * CT) + CT)
                nc.scalar.activation(p_hi[:, m, :], stage[:, m, :], ACT.Copy).then_inc(s_phi, 1)

            def v_part(b, m):
                act.wait_ge(s_unit, b * UNITS + V0 + m + 1)
                part_hi(v_hi[:, m, :], ring[:, (V0 + m) % RING, :]).then_inc(s_vhi, 1)

            def image(b, par, more):
                for j in range(NB * CT):
                    half, i = j // CT, j % CT
                    act.wait_ge(s_unit, b * UNITS + T0 + j + 1)
                    part_hi(t_hi[:, i, half * HALF:(half + 1) * HALF], ring[:, (T0 + j) % RING, :],
                            t_bias[:, i:i + 1]).then_inc(s_thi, 1)
                    if j == 0:
                        act.wait_ge(s_hdot, b * CT + CT)
                        nc.scalar.activation(dot_part[0], h_dot, ACT.Copy).then_inc(s_dpart[0], 1)
                    if j == 2:
                        act.wait_ge(s_drest, b + 1)
                        nc.scalar.activation(dot_part[1], h_dot, ACT.Copy).then_inc(s_dpart[1], 1)
                act.wait_ge(s_kb, b + 1)
                nc.scalar.activation(keybias[:, :], ps_keybias, ACT.Identity, bias=bqk[:, :]).then_inc(s_kbc, 1)
                act.wait_ge(s_kbc, b + 1)
                copy_scores(b, 0)
                for m in range(2):
                    v_part(b, m)
                for m in range(MT):
                    exponential(b, 0, m)
                    if m + 2 < MT:
                        v_part(b, m + 2)
                    p_part(b, 0, m)
                copy_scores(b, 1)
                exponential(b, 1, 0)
                for m in range(MT):
                    if m + 1 < MT:
                        exponential(b, 1, m + 1)
                    p_part(b, 1, m)
                if more:
                    for k in range(CT):
                        normed(b + 1, 1 - par, k)

            with act.Fori(0, B - 3, 2) as b:
                image(b, 0, True)
                image(b + 1, 1, True)
            image(B - 2, 0, True)
            image(B - 1, 1, False)

        @block.gpsimd
        def _(pool):
            nc.gpsimd.memset(minus_half[:, :], -0.5).then_inc(s_half, 1)
            pool.wait_ge(s_half, 1)
            pool.wait_ge(s_bb, 2)
            nc.gpsimd.partition_all_reduce(bqk[:, :], bb_sum[:, :], P, bass.bass_isa.ReduceOp.add).then_inc(s_bqk, 1)

            def inverse_deviation(n):
                pool.wait_ge(s_norm, n * NORM + 5)
                nc.gpsimd.tensor_tensor(rstd[:, :], veps[:, :], minus_half[:, :], ALU.pow).then_inc(s_rstd, 1)

            def h_part(n, k):
                pool.wait_ge(s_hf, n * CT + k + 1)
                pool.wait_ge(s_hhi, n * CT + k + 1)
                nc.gpsimd.tensor_tensor(h_lo[:, k, :], h_full[k % 2], h_hi[:, k, :].bitcast(FP32),
                                        ALU.subtract).then_inc(s_hlo, 1)

            def over_partitions(b, nb, op, ready, done):
                lone_wait(pool, ready, b * 2 + nb + 1)
                nc.gpsimd.partition_all_reduce(colall[:, :], colpart[:, :], P, op).then_inc(done, 1)

            def weight_rest(k):
                pool.wait_ge(s_whi, CT + k + 1)
                nc.gpsimd.tensor_tensor(w_lo[1][:, 2 * k:2 * k + 2, :], raw[:, k, :, :],
                                        w_hi[1][:, 2 * k:2 * k + 2, :].bitcast(FP32), ALU.subtract).then_inc(s_wlo[1], 1)

            for k in range(CT):
                weight_rest(k)
                if k == 1:
                    inverse_deviation(0)
            for k in range(CT):
                h_part(0, k)

            def image(b, more):
                over_partitions(b, 0, bass.bass_isa.ReduceOp.max, s_maxp, s_maxall)
                over_partitions(b, 0, bass.bass_isa.ReduceOp.add, s_sump, s_sumall)
                over_partitions(b, 1, bass.bass_isa.ReduceOp.max, s_maxp, s_maxall)
                if more:
                    inverse_deviation(b + 1)
                    for k in range(CT):
                        h_part(b + 1, k)
                over_partitions(b, 1, bass.bass_isa.ReduceOp.add, s_sump, s_sumall)

            with pool.Fori(0, B - 1) as b:
                image(b, True)
            image(B - 1, False)

        @block.vector
        def _(dve):
            nc.vector.memset(ones[:, :], 1.0).then_inc(s_ones, 1)
            nc.vector.memset(ones_bf[:, :], 1.0).then_inc(s_ones, 1)
            dve.wait_ge(s_col, 2 * DMA)
            nc.vector.tensor_tensor(bb[:, :], col[:, BQ:BQ + CT], col[:, BK:BK + CT], ALU.mult).then_inc(s_bb, 1)
            dve.wait_ge(s_bb, 1)
            nc.vector.tensor_reduce(bb_sum[:, :], bb[:, :], AX.X, ALU.add).then_inc(s_bb, 1)

            def weight_rest(k):
                dve.wait_ge(s_whi, k + 1)
                nc.vector.tensor_tensor(w_lo[0][:, 2 * k:2 * k + 2, :], raw[:, k, :, :],
                                        w_hi[0][:, 2 * k:2 * k + 2, :].bitcast(FP32), ALU.subtract).then_inc(s_wlo[0], 1)

            def weighted_rows(v, w, side, bias, k):
                dve.wait_ge(s_w[w][k], 2 * DMA)
                rows, by = raw[:, k, side, :], col[:, bias + k:bias + k + 1]
                if k == 0:
                    a = nc.vector.tensor_scalar(weighted[v], rows, by, None, ALU.mult)
                else:
                    dve.wait_ge(s_weighted[v], k)
                    a = nc.vector.scalar_tensor_tensor(weighted[v], rows, by, weighted[v], ALU.mult, ALU.add)
                a.then_inc(s_weighted[v], 1)

            def product_rest(w, i):
                dve.wait_ge(s_prod_hi, w * CT + (i if w == 0 else (i + 1) % CT) + 1)
                nc.vector.tensor_tensor(product_lo[w][:, i, :], product_bank[w][i],
                                        product_hi[w][:, i, :].bitcast(FP32), ALU.subtract).then_inc(s_prod_lo, 1)

            def channel_stats(n, par, loaded=None):
                if loaded is not None:
                    dve.wait_ge(s_x[par], loaded)
                for k in range(CT):
                    if loaded is None:
                        dve.wait_ge(s_first[k], DMA)
                    for s in range(NB):
                        nc.vector.bn_stats(stats[:, k, s, :],
                                           xs[:, par, k, s * HALF:(s + 1) * HALF]).then_inc(s_stats, 1)
                lone_wait(dve, s_stats, (n + 1) * (CT * NB))
                for k in range(CT):
                    nc.vector.bn_aggr(mv[:, k, :], stats[:, k, :, :].rearrange("p s e -> p (s e)")).then_inc(s_aggr, 1)

            def about_mean(n):
                at = n * NORM
                dve.wait_ge(s_mean, n + 1)
                nc.vector.tensor_copy(gmean[:, :], ps_mean).then_inc(s_norm, 1)
                nc.vector.tensor_tensor(dmean[:, :], ps_mean, mv[:, :, 0], ALU.subtract).then_inc(s_norm, 1)
                dve.wait_ge(s_norm, at + 2)
                nc.vector.tensor_tensor(shift[:, :], dmean[:, :], dmean[:, :], ALU.mult).then_inc(s_norm, 1)
                dve.wait_ge(s_norm, at + 3)
                nc.vector.tensor_tensor(spread[:, :], shift[:, :], mv[:, :, 1], ALU.add).then_inc(s_norm, 1)

            def variance(n):
                dve.wait_ge(s_var, n + 1)
                nc.vector.tensor_scalar(veps[:, :], ps_var, EPS, None, ALU.add).then_inc(s_norm, 1)

            def affine(n, step):
                if step == 0:
                    dve.wait_ge(s_rstd, n + 1)
                    a = nc.vector.tensor_tensor(h_scale[:, :], rstd[:, :], col[:, GW:GW + CT], ALU.mult)
                else:
                    dve.wait_ge(s_norm, n * NORM + 5 + step)
                    if step == 1:
                        a = nc.vector.tensor_tensor(shift[:, :], h_scale[:, :], gmean[:, :], ALU.mult)
                    else:
                        a = nc.vector.tensor_tensor(h_bias[:, :], col[:, GB:GB + CT], shift[:, :], ALU.subtract)
                a.then_inc(s_norm, 1)

            def dot_step(n, k):
                dve.wait_ge(s_hf, n * CT + k + 1)
                if k == 0:
                    nc.vector.tensor_scalar(h_dot, h_full[0], k_dir[:, 0:1], None, ALU.mult).then_inc(s_hdot, 1)
                else:
                    dve.wait_ge(s_hdot, n * CT + k)
                    nc.vector.scalar_tensor_tensor(h_dot, h_full[k % 2], k_dir[:, k:k + 1], h_dot, ALU.mult,
                                                   ALU.add).then_inc(s_hdot, 1)

            def dot_rest(n):
                dve.wait_ge(s_dpart[0], n + 1)
                nc.vector.tensor_tensor(h_dot, h_dot, dot_part[0], ALU.subtract).then_inc(s_drest, 1)

            def dot_last(n):
                dve.wait_ge(s_dpart[1], n + 1)
                nc.vector.tensor_tensor(dot_part[2], h_dot, dot_part[1], ALU.subtract).then_inc(s_dpart[2], 1)

            for k in range(CT):
                weight_rest(k)
                weighted_rows(0, 0, 0, BQ, k)
                weighted_rows(1, 0, 1, BK, k)
            channel_stats(0, 0)
            dve.wait_ge(s_vec, 2)
            nc.vector.tensor_copy(k_dir[:, :], ps_kd).then_inc(s_vec_sb, 1)
            nc.vector.tensor_copy(t_bias[:, :], ps_tb).then_inc(s_vec_sb, 1)
            for i in range(CT):
                product_rest(0, i)
            dve.wait_ge(s_vec_sb, 2)
            about_mean(0)
            variance(0)
            for step in range(3):
                affine(0, step)
            for k in range(CT):
                dot_step(0, k)
                weighted_rows(2, 1, 1, BV, k)
            product_rest(1, 3)
            for i in range(CT - 1):
                product_rest(1, i)
            dve.wait_ge(s_vec, 3)
            nc.vector.tensor_tensor(out_bias[:, :], ps_ob, col[:, BO:BO + CT], ALU.add).then_inc(s_vec_sb, 1)
            dve.wait_ge(s_vec_sb, 3)

            def over_tiles(b, nb, first, op, ready, half_done, done):
                if first:
                    dve.wait_ge(ready, b * (2 * MT) + MT * nb + MT // 2)
                    nc.vector.tensor_reduce(stage[:, MT, :], stage[:, 0:MT // 2, :].rearrange("p s n -> p n s"),
                                            AX.X, op).then_inc(half_done, 1)
                else:
                    dve.wait_ge(ready, b * (2 * MT) + MT * (nb + 1))
                    dve.wait_ge(half_done, b * 2 + nb + 1)
                    nc.vector.tensor_reduce(colpart[:, :], stage[:, MT // 2:MT + 1, :].rearrange("p s n -> p n s"),
                                            AX.X, op).then_inc(done, 1)

            def key_max(b, nb, first):
                over_tiles(b, nb, first, ALU.max, s_copied, s_maxh, s_maxp)

            def key_sum(b, nb, first):
                over_tiles(b, nb, first, ALU.add, s_exp, s_sumh, s_sump)

            def subtract_max(b, nb, m):
                if m == 0:
                    dve.wait_ge(s_maxall, b * 2 + nb + 1)
                nc.vector.tensor_tensor(stage[:, m, :], stage[:, m, :], colall[:, :], ALU.subtract).then_inc(s_sub, 1)

            def p_rest(b, nb, m):
                dve.wait_ge(s_phi, b * (2 * MT) + MT * nb + m + 1)
                nc.vector.tensor_tensor(p_lo[:, m, :], stage[:, m, :], p_hi[:, m, :].bitcast(FP32),
                                        ALU.subtract).then_inc(s_plo, 1)

            def v_rest(b, m):
                dve.wait_ge(s_vhi, b * 8 + m + 1)
                nc.vector.tensor_tensor(v_lo[:, m, :], ring[:, (V0 + m) % RING, :], v_hi[:, m, :].bitcast(FP32),
                                        ALU.subtract).then_inc(s_vlo, 1)

            def inverse(b, nb):
                dve.wait_ge(s_sumall, b * 2 + nb + 1)
                nc.vector.reciprocal(inv[:, :], colall[:, :]).then_inc(s_inv, 1)

            def scale_output(b, nb, c):
                dve.wait_ge(s_inv, b * 2 + nb + 1)
                dve.wait_ge(s_bank, b * (2 * CT) + CT * nb + c + 1)
                if c == 3:
                    dve.wait_ge(s_result, b * (2 * CT) + CT * nb + 1)
                nc.vector.tensor_tensor(scaled_at[c % 3], av[:, c, :], inv[:, :], ALU.mult).then_inc(s_scaled, 1)

            def add_input(b, par, nb, c):
                dve.wait_ge(s_scaled, b * (2 * CT) + CT * nb + c + 1)
                here = xs[:, par, c, nb * HALF:(nb + 1) * HALF]
                nc.vector.scalar_tensor_tensor(here, scaled_at[c % 3], out_bias[:, c:c + 1], here, ALU.add,
                                               ALU.add).then_inc(s_result, 1)

            def image(b, par, more):
                for j in range(NB * CT):
                    half, i = j // CT, j % CT
                    here = slice(half * HALF, (half + 1) * HALF)
                    dve.wait_ge(s_thi, b * 8 + j + 1)
                    nc.vector.scalar_tensor_tensor(t_lo[:, i, here], ring[:, (T0 + j) % RING, :], t_bias[:, i:i + 1],
                                                   t_hi[:, i, here].bitcast(FP32), ALU.add,
                                                   ALU.subtract).then_inc(s_tlo, 1)
                    if j == 1:
                        dot_rest(b)
                    if j == 3:
                        dot_last(b)
                key_max(b, 0, True)
                key_max(b, 0, False)
                for m in range(2):
                    v_rest(b, m)
                for m in range(MT):
                    subtract_max(b, 0, m)
                    if m >= 1:
                        p_rest(b, 0, m - 1)
                    if m + 2 < MT:
                        v_rest(b, m + 2)
                    if m == MT // 2:
                        key_sum(b, 0, True)
                p_rest(b, 0, MT - 1)
                key_sum(b, 0, False)
                dve.wait_ge(s_sump, b * 2 + 1)
                key_max(b, 1, True)
                inverse(b, 0)
                if more:
                    channel_stats(b + 1, 1 - par, (b - par) * (DMA // 2) + DMA)
                key_max(b, 1, False)
                if more:
                    about_mean(b + 1)
                subtract_max(b, 1, 0)
                subtract_max(b, 1, 1)
                for m in range(2, MT):
                    subtract_max(b, 1, m)
                    if more and m >= MT - 2:
                        affine(b + 1, 2 * (m - MT + 2))
                    if m < MT - 1:
                        p_rest(b, 1, m - 2)
                    if more and m == MT - 2:
                        affine(b + 1, 1)
                    if more and m == 4:
                        variance(b + 1)
                key_sum(b, 1, True)
                for c in range(3):
                    scale_output(b, 0, c)
                add_input(b, par, 0, 0)
                scale_output(b, 0, 3)
                add_input(b, par, 0, 1)
                add_input(b, par, 0, 2)
                p_rest(b, 1, MT - 3)
                dve.wait_ge(s_result, b * (2 * CT) + 3)
                key_sum(b, 1, False)
                if more:
                    dve.wait_ge(s_sump, b * 2 + 2)
                    dve.wait_ge(s_plo, b * (2 * MT) + 2 * MT - 2)
                    dot_step(b + 1, 0)
                    dot_step(b + 1, 1)
                p_rest(b, 1, MT - 2)
                p_rest(b, 1, MT - 1)
                add_input(b, par, 0, 3)
                if more:
                    dot_step(b + 1, 2)
                    dot_step(b + 1, 3)
                inverse(b, 1)
                if more:
                    for c in range(3):
                        scale_output(b, 1, c)
                    add_input(b, par, 1, 0)
                    scale_output(b, 1, 3)
                    for c in range(1, CT):
                        add_input(b, par, 1, c)
                else:
                    for c in range(CT):
                        scale_output(b, 1, c)
                        add_input(b, par, 1, c)

            with dve.Fori(0, B - 3, 2) as b:
                image(b, 0, True)
                image(b + 1, 1, True)
            image(B - 2, 0, True)
            image(B - 1, 1, False)


def kernel(x, L0_conv_gn_w, L0_conv_gn_b, L0_conv_qkv_w, L0_conv_qkv_b, L0_conv_out_w, L0_conv_out_b):
    import concourse.bacc as bacc
    from concourse.bass_utils import run_bass_kernel_spmd

    rows = np.concatenate([np.asarray(a).reshape(-1, P) for a in
                           (L0_conv_qkv_b, L0_conv_gn_w, L0_conv_gn_b, L0_conv_out_b)])
    arrays = {
        "x_in": np.ascontiguousarray(x).reshape(B, C, N),
        "wq": np.ascontiguousarray(L0_conv_qkv_w[0:C]),
        "wk": np.ascontiguousarray(L0_conv_qkv_w[C:2 * C]),
        "wv": np.ascontiguousarray(L0_conv_qkv_w[2 * C:3 * C]),
        "wo_t": np.ascontiguousarray(np.asarray(L0_conv_out_w).T),
        "cols": np.ascontiguousarray(rows.T),
        "block_avg": np.kron(np.eye(P * GROUPS // C), np.full((C // GROUPS,) * 2, GROUPS / C)).astype(np.float32),
    }
    nc = bacc.Bacc("TRN2", target_bir_lowering=False, num_devices=1, dynamic_dma_scratch_size=1024)
    ins = [nc.dram_tensor(n, a.shape, mybir.dt.from_np(a.dtype), kind="ExternalInput").ap() for n, a in arrays.items()]
    out = nc.dram_tensor("out", (B, C, N), FP32, kind="ExternalOutput").ap()
    attention_kernel(nc, *ins, out)
    r = run_bass_kernel_spmd(nc, [arrays], core_ids=[0])
    return r.results[0]["out"].reshape(B, C, H, W)
```

```python
from contextlib import ExitStack

import numpy as np

import concourse.bass as bass
from concourse import mybir


FP32 = mybir.dt.float32
FP32R = mybir.dt.float32r
BF16 = mybir.dt.bfloat16
ALU = mybir.AluOpType
ACT = mybir.ActivationFunctionType
AX = mybir.AxisListType

P = 128
B, C, H, W = 16, 512, 32, 32
N = H * W
GROUPS = 32
EPS = 1e-5
SCALE = 1.0 / float(C) ** 0.5
CT = C // P
MT = N // P
HALF = 512
NB = N // HALF
RING = 3
UNITS = NB * CT + MT + NB * MT
DMA = 16

T0 = 0
S0 = T0 + NB * CT
V0 = S0 + MT
S1 = V0 + MT
SCORES = (S0, S1)
BQ, BK, BV, GW, GB, BO = (CT * i for i in range(6))


def attention_kernel(nc, x, wq, wk, wv, wo_t, cols, block_avg, out):
    x_v = x.rearrange("b (k p) n -> b p k n", p=P)
    out_v = out.rearrange("b (k p) n -> b p k n", p=P)
    w_v = [[w.rearrange("(k p) n -> p k n", p=P) for w in pair] for pair in ((wk, wq), (wv, wo_t))]

    ctx = ExitStack()
    with ctx:
        def sb(name, shape, dt=FP32):
            return ctx.enter_context(nc.sbuf_tensor(name, shape, dt))

        def ps(name, shape):
            return ctx.enter_context(nc.psum_tensor(name, shape, FP32))

        def sem(name):
            return ctx.enter_context(nc.semaphore(name))

        xs = sb("xs", [P, 2, CT, N])
        h_hi, h_lo = (sb(f"h_{s}", [P, CT, N], FP32R) for s in ("hi", "lo"))
        t_hi, t_lo = (sb(f"t_{s}", [P, CT, N], FP32R) for s in ("hi", "lo"))
        v_hi, v_lo = (sb(f"v_{s}", [P, MT, C], FP32R) for s in ("hi", "lo"))
        p_hi, p_lo = (sb(f"p_{s}", [P, MT, HALF], FP32R) for s in ("hi", "lo"))
        g_hi, g_lo = (sb(f"g_{s}", [P, CT, C], FP32R) for s in ("hi", "lo"))
        u_hi, u_lo = (sb(f"u_{s}", [P, CT, C], FP32R) for s in ("hi", "lo"))
        stage = sb("stage", [P, MT + 1, HALF])
        colpart = sb("colpart", [P, HALF])
        colall = sb("colall", [P, HALF])
        inv = sb("inv", [P, HALF])
        scaled = sb("scaled", [P, 2, HALF])
        col = sb("col", [P, 6 * CT])
        avg = sb("avg", [P, P])
        ones, ones_bf = sb("ones", [P, 1]), sb("ones_bf", [P, 1], BF16)
        stats = sb("stats", [P, CT, NB, 6])
        mv = sb("mv", [P, CT, 2])
        gmean, dmean, spread, veps, rstd, h_scale, shift, h_bias, minus_half = (
            sb(n, [P, CT]) for n in ("gmean", "dmean", "spread", "veps", "rstd", "h_scale", "shift", "h_bias",
                                     "minus_half"))
        keybias = sb("keybias", [P, MT])
        t_bias, k_dir, out_bias = (sb(n, [P, CT]) for n in ("t_bias", "k_dir", "out_bias"))
        bb, bb_sum, bqk = sb("bb", [P, CT]), sb("bb_sum", [P, 1]), sb("bqk", [P, 1])

        ring = ps("ring", [P, RING, HALF])
        av = ps("av", [P, CT, HALF])
        small = ps("small", [P, HALF])
        ps_keybias = small[:, 0:MT]
        ps_mean, ps_var, ps_kd, ps_tb, ps_ob = (small[:, c:c + CT] for c in (16, 24, 32, 40, 48))

        raw = xs[:, 1, :, :].rearrange("p k n -> p (k n)").rearrange("p (k w n) -> p k w n", k=CT, w=2)
        w_hi, w_lo = (p_hi, v_hi), (p_lo, v_lo)
        product_hi, product_lo = (g_hi, u_hi), (g_lo, u_lo)
        product_bank = ([ring[:, 0, :], ring[:, 1, :], ring[:, 2, :], av[:, 0, :]],
                        [av[:, 1, :], av[:, 2, :], av[:, 3, :], av[:, 0, :]])
        product_order = (3, 0, 1, 2)
        h_full = [stage[:, 2 * q:2 * q + 2, :].rearrange("p a n -> p (a n)") for q in range(2)]
        first_full = h_full + [xs[:, 1, 0, :], xs[:, 1, 1, :]]
        h_dot = stage[:, 4:6, :].rearrange("p a n -> p (a n)")
        dot_part = [stage[:, 6 + i, :].bitcast(BF16) for i in range(3)]
        weighted = [scaled[:, 0, :], scaled[:, 1, :], inv[:, :]]
        scaled_at = [scaled[:, 0, :], scaled[:, 1, :], colpart[:, :], colall[:, :]]

        s_col = sem("cols_loaded")
        s_w = [[sem(f"weights{w}_loaded{k}") for k in range(CT)] for w in range(2)]
        s_first = [sem(f"first_image_loaded{k}") for k in range(CT)]
        s_x = [sem(f"x_loaded{i}") for i in range(2)]
        s_stored = [sem(f"stored{i}") for i in range(2)]
        s_ones = sem("ones_set")
        s_half = sem("minus_half_set")
        s_whi = sem("weights_hi_done")
        s_wlo = [sem(f"weights{w}_lo_done") for w in range(2)]
        s_weighted = [sem(f"rows_weighted{v}") for v in range(3)]
        s_chunk = [None] + [sem(f"chunk_weighted{v}") for v in (1, 2)]
        s_prod = sem("weight_product_done")
        s_prod_hi, s_prod_lo = sem("product_hi_done"), sem("product_lo_done")
        s_bb, s_bqk = sem("bias_dot_step"), sem("bias_dot_done")
        s_vec = sem("weight_vector_done")
        s_vec_sb = sem("weight_vectors_copied")
        s_unit = sem("unit_done")
        s_kb = sem("keybias_summed")
        s_kbc = sem("keybias_copied")
        s_mean, s_var = sem("group_mean_done"), sem("group_var_done")
        s_pused = sem("p_tile_used")
        s_bank = sem("av_bank_done")
        s_thi, s_tlo = sem("t_hi_done"), sem("t_lo_done")
        s_vhi, s_vlo = sem("v_hi_done"), sem("v_lo_done")
        s_copied = sem("scores_copied")
        s_sub = sem("max_subtracted")
        s_exp = sem("exp_done")
        s_phi, s_plo = sem("p_hi_done"), sem("p_lo_done")
        s_maxh, s_maxp = sem("max_first_tiles"), sem("max_by_partition")
        s_sumh, s_sump = sem("sum_first_tiles"), sem("sum_by_partition")
        s_maxall, s_sumall = sem("max_all"), sem("sum_all")
        s_inv = sem("inverse_done")
        s_scaled, s_result = sem("output_scaled"), sem("result_done")
        s_stats, s_aggr = sem("stats_done"), sem("channel_stats_done")
        s_norm = sem("norm_step")
        s_rstd = sem("rstd_done")
        s_hf, s_hhi, s_hlo = sem("h_full_done"), sem("h_hi_done"), sem("h_lo_done")
        s_hdot = sem("h_dot_step")
        s_dpart = [sem(f"dot_part{i}_done") for i in range(3)]
        s_drest = sem("dot_rest_done")
        s_carrier = sem("wait_carrier")
        NORM = 8

        def lone_wait(eng, sem, count):
            eng.wait_ge(sem, count)
            eng.sem_inc(s_carrier, 1)

        block = ctx.enter_context(nc.Block())

        @block.sync
        def _(sp):
            def load_weights(w, k):
                for i in range(2):
                    sp.dma_start(raw[:, k, i, :], w_v[w][i][:, k, :]).then_inc(s_w[w][k], DMA)

            load_weights(0, 0)
            sp.dma_start(col[:, :], cols).then_inc(s_col, DMA)
            sp.dma_start(avg[:, :], block_avg).then_inc(s_col, DMA)
            for k in range(1, CT):
                load_weights(0, k)
            for k in range(CT):
                sp.dma_start(xs[:, 0, k, :], x_v[0, :, k, :]).then_inc(s_first[k], DMA)
            for k in range(CT):
                sp.wait_ge(s_wlo[0], k + 1)
                sp.wait_ge(s_weighted[0], k + 1)
                sp.wait_ge(s_weighted[1], k + 1)
                load_weights(1, k)
            sp.wait_ge(s_wlo[1], CT)
            sp.wait_ge(s_weighted[2], CT)
            sp.wait_ge(s_hlo, CT)
            sp.wait_ge(s_hdot, CT)
            sp.dma_start(xs[:, 1, :, :], x_v[1]).then_inc(s_x[1], DMA)

            def image(b, par, load, last=False):
                for nb in range(NB):
                    if last and nb == NB - 1:
                        for c in range(CT):
                            sp.wait_ge(s_result, b * (2 * CT) + CT * nb + c + 1)
                            sp.dma_start(out_v[b, :, c, nb * HALF:(nb + 1) * HALF],
                                         xs[:, par, c, nb * HALF:(nb + 1) * HALF]).then_inc(s_stored[par], DMA)
                        continue
                    sp.wait_ge(s_result, b * (2 * CT) + CT * (nb + 1))
                    sp.dma_start(out_v[b, :, :, nb * HALF:(nb + 1) * HALF],
                                 xs[:, par, :, nb * HALF:(nb + 1) * HALF]).then_inc(s_stored[par], DMA)
                if load:
                    sp.wait_ge(s_stored[par], (b - par) * DMA + 2 * DMA)
                    sp.dma_start(xs[:, par, :, :], x_v[b + 2]).then_inc(s_x[par], DMA)

            with sp.Fori(0, B - 3, 2) as b:
                image(b, 0, True)
                image(b + 1, 1, True)
            image(B - 2, 0, False)
            image(B - 1, 1, False, last=True)
            sp.wait_ge(s_stored[0], B // 2 * 2 * DMA)
            sp.wait_ge(s_stored[1], (B // 2 * 2 - 1 + CT) * DMA)

        @block.tensor
        def _(pe):
            def three(ps_out, st_hi, st_lo, m_hi, m_lo, first, last):
                nc.tensor.matmul(ps_out, st_hi, m_hi, start=first, stop=False)
                nc.tensor.matmul(ps_out, st_hi, m_lo, start=False, stop=False)
                return nc.tensor.matmul(ps_out, st_lo, m_hi, start=False, stop=last)

            def unit(j, stat, mov):
                for k in range(CT):
                    a = three(ring[:, j % RING, :], *stat(k), *mov(k), k == 0, k == CT - 1)
                a.then_inc(s_unit, 1)

            def weight_product(w, k, during={}):
                pe.wait_ge(s_wlo[w], k + 1)
                for i in range(CT):
                    if i in during:
                        during[i]()
                    if w and k == 0 and i == CT - 1:
                        pe.wait_ge(s_prod_lo, 1)
                    cs = slice(i * P, (i + 1) * P)
                    a = three(product_bank[w][i], w_hi[w][:, 2 * k, cs], w_lo[w][:, 2 * k, cs],
                              w_hi[w][:, 2 * k + 1, :], w_lo[w][:, 2 * k + 1, :], k == 0, k == CT - 1)
                    if k == CT - 1:
                        a.then_inc(s_prod, 1)

            def weight_vector(v, dst):
                pe.wait_ge(s_weighted[v], CT)
                for i in range(CT):
                    a = nc.tensor.matmul(dst[:, i:i + 1], weighted[v][:, i * P:(i + 1) * P], ones[:, :],
                                         start=True, stop=True)
                a.then_inc(s_vec, 1)

            def group_mean(n):
                pe.wait_ge(s_aggr, n * CT + CT)
                nc.tensor.matmul(ps_mean, avg[:, :], mv[:, :, 0], start=True, stop=True).then_inc(s_mean, 1)

            def group_var(n):
                pe.wait_ge(s_norm, n * NORM + 4)
                nc.tensor.matmul(ps_var, avg[:, :], spread[:, :], start=True, stop=True).then_inc(s_var, 1)

            for k in range(CT):
                weight_product(0, k)
            pe.wait_ge(s_ones, 2)
            weight_vector(0, ps_kd)
            weight_vector(1, ps_tb)

            def first_mean():
                pe.wait_ge(s_vec_sb, 2)
                pe.wait_ge(s_col, 2 * DMA)
                group_mean(0)

            weight_product(1, 0, {1: first_mean, 3: lambda: group_var(0)})
            weight_product(1, 1)
            weight_product(1, 2)
            pe.wait_ge(s_norm, 5)
            weight_vector(2, ps_ob)
            weight_product(1, 3)
            pe.wait_ge(s_vec_sb, 3)
            pe.wait_ge(s_prod_lo, CT)

            def output_half(b, nb, during={}, last=False):
                ending = 3 if last else 0
                steps = [(m, c) for m in range(MT - ending) for c in range(CT)]
                steps += [(m, c) for c in range(CT) for m in range(MT - ending, MT)]
                for m, c in steps:
                    if c == 0:
                        if m in during:
                            during[m]()
                        pe.wait_ge(s_plo, b * (2 * MT) + MT * nb + m + 1)
                    if nb == 1 and m == 0:
                        pe.wait_ge(s_scaled, b * (2 * CT) + c + 1)
                    cs = slice(c * P, (c + 1) * P)
                    a = three(av[:, c, :], v_hi[:, m, cs], v_lo[:, m, cs], p_hi[:, m, :], p_lo[:, m, :],
                              m == 0, m == MT - 1)
                    if m == MT - 1:
                        a.then_inc(s_bank, 1)
                    elif nb == 0 and c == CT - 1:
                        a.then_inc(s_pused, 1)

            def image(b, more):
                pe.wait_ge(s_hlo, b * CT + CT)
                for j in range(NB * CT):
                    half, i = j // CT, j % CT
                    if j >= RING:
                        pe.wait_ge(s_tlo, b * 8 + j - RING + 1)
                    unit(T0 + j,
                         lambda k: (g_hi[:, k, i * P:(i + 1) * P], g_lo[:, k, i * P:(i + 1) * P]),
                         lambda k: (h_hi[:, k, half * HALF:(half + 1) * HALF],
                                    h_lo[:, k, half * HALF:(half + 1) * HALF]))
                    if j == CT + 1:
                        for part in range(3):
                            pe.wait_ge(s_dpart[part], b + 1)
                        for m in range(MT):
                            for part in range(3):
                                a = nc.tensor.matmul(ps_keybias[:, m:m + 1], dot_part[part][:, m * P:(m + 1) * P],
                                                     ones_bf[:, :], start=part == 0, stop=part == 2)
                        a.then_inc(s_kb, 1)

                def scores(nb):
                    for m in range(MT):
                        j = SCORES[nb] + m
                        if nb == 0 and m in (0, CT):
                            pe.wait_ge(s_tlo, b * 8 + m + CT)
                        if nb == 0 and m < RING:
                            pe.wait_ge(s_tlo, b * 8 + 8 - RING + m + 1)
                        elif nb == 1 and m < RING:
                            pe.wait_ge(s_vlo, b * 8 + 8 - RING + m + 1)
                        else:
                            pe.wait_ge(s_copied, b * (2 * MT) + MT * nb + m - RING + 1)
                        unit(j,
                             lambda k: (t_hi[:, k, m * P:(m + 1) * P], t_lo[:, k, m * P:(m + 1) * P]),
                             lambda k: (h_hi[:, k, nb * HALF:(nb + 1) * HALF],
                                        h_lo[:, k, nb * HALF:(nb + 1) * HALF]))

                scores(0)
                pe.wait_ge(s_prod_lo, 2 * CT)
                for m in range(MT):
                    if m < RING:
                        pe.wait_ge(s_copied, b * (2 * MT) + MT - RING + m + 1)
                    else:
                        pe.wait_ge(s_vlo, b * 8 + m - RING + 1)
                    unit(V0 + m,
                         lambda k: (h_hi[:, k, m * P:(m + 1) * P], h_lo[:, k, m * P:(m + 1) * P]),
                         lambda k: (u_hi[:, k, :], u_lo[:, k, :]))
                scores(1)
                pe.wait_ge(s_vlo, b * 8 + 8)
                output_half(b, 0, {2: lambda: group_mean(b + 1), 4: lambda: group_var(b + 1)} if more else {})
                output_half(b, 1, last=not more)

            with pe.Fori(0, B - 1) as b:
                image(b, True)
            image(B - 1, False)

        @block.scalar
        def _(act):
            def part_hi(out, ps_in, bias=0.0):
                return nc.scalar.activation(out, ps_in, ACT.Identity, bias=bias)

            def weight_part(w, k):
                act.wait_ge(s_w[w][k], 2 * DMA)
                nc.scalar.activation(w_hi[w][:, 2 * k:2 * k + 2, :], raw[:, k, :, :], ACT.Copy).then_inc(s_whi, 1)

            def product_part(w, i):
                act.wait_ge(s_prod, w * CT + i + 1)
                part_hi(product_hi[w][:, i, :], product_bank[w][i]).then_inc(s_prod_hi, 1)

            def normed(n, par, k):
                if k == 0:
                    act.wait_ge(s_norm, n * NORM + NORM)
                    act.wait_ge(s_sumh, n * 2)
                    act.wait_ge(s_plo, n * (2 * MT) - MT // 2)
                elif k >= 2:
                    act.wait_ge(s_hlo, n * CT + k - 1)
                    act.wait_ge(s_hdot, n * CT + k - 1)
                for out, done in ((h_full[k % 2], s_hf), (h_hi[:, k, :], s_hhi)):
                    nc.scalar.activation(out, xs[:, par, k, :], ACT.Identity, bias=h_bias[:, k:k + 1],
                                         scale=h_scale[:, k:k + 1]).then_inc(done, 1)

            for k in range(CT):
                weight_part(0, k)
            weight_part(1, 0)
            product_part(0, product_order[0])
            weight_part(1, 1)
            for i in product_order[1:]:
                product_part(0, i)
            weight_part(1, 2)
            weight_part(1, 3)
            act.wait_ge(s_norm, NORM)
            for k in range(CT):
                if k >= 2:
                    act.wait_ge(s_wlo[1], k - 1)
                    act.wait_ge(s_weighted[2], k - 1)
                nc.scalar.activation(first_full[k], xs[:, 0, k, :], ACT.Identity, bias=h_bias[:, k:k + 1],
                                     scale=h_scale[:, k:k + 1]).then_inc(s_hf, 1)
            act.wait_ge(s_hf, CT)
            act.wait_ge(s_hhi, CT - 1)
            nc.scalar.activation(h_hi[:, CT - 1, :], first_full[CT - 1], ACT.Copy).then_inc(s_hhi, 1)
            for i in product_order:
                product_part(1, i)
            act.wait_ge(s_vec_sb, 2)
            act.wait_ge(s_bqk, 1)

            def copy_scores(b, nb):
                for m in range(MT):
                    act.wait_ge(s_unit, b * UNITS + SCORES[nb] + m + 1)
                    if nb == 1 and m in (0, MT // 2):
                        act.wait_ge(s_plo, b * (2 * MT) + m + MT // 2)
                        act.wait_ge(s_sumh if m == 0 else s_sump, b * 2 + 1)
                    nc.scalar.activation(stage[:, m, :], ring[:, (SCORES[nb] + m) % RING, :], ACT.Identity,
                                         bias=keybias[:, m:m + 1]).then_inc(s_copied, 1)

            def exponential(b, nb, m):
                act.wait_ge(s_sub, b * (2 * MT) + MT * nb + m + 1)
                nc.scalar.activation(stage[:, m, :], stage[:, m, :], ACT.Exp, scale=SCALE).then_inc(s_exp, 1)

            def p_part(b, nb, m):
                act.wait_ge(s_exp, b * (2 * MT) + MT * nb + m + 1)
                if nb == 1:
                    if m < MT - 1:
                        act.wait_ge(s_pused, b * (MT - 1) + m + 1)
                    else:
                        act.wait_ge(s_bank, b * (2 * CT) + CT)
                nc.scalar.activation(p_hi[:, m, :], stage[:, m, :], ACT.Copy).then_inc(s_phi, 1)

            def v_part(b, m):
                act.wait_ge(s_unit, b * UNITS + V0 + m + 1)
                part_hi(v_hi[:, m, :], ring[:, (V0 + m) % RING, :]).then_inc(s_vhi, 1)

            def image(b, par, more):
                for j in range(NB * CT):
                    half, i = j // CT, j % CT
                    act.wait_ge(s_unit, b * UNITS + T0 + j + 1)
                    part_hi(t_hi[:, i, half * HALF:(half + 1) * HALF], ring[:, (T0 + j) % RING, :],
                            t_bias[:, i:i + 1]).then_inc(s_thi, 1)
                    if j == 0:
                        act.wait_ge(s_hdot, b * CT + CT)
                        nc.scalar.activation(dot_part[0], h_dot, ACT.Copy).then_inc(s_dpart[0], 1)
                    if j == 2:
                        act.wait_ge(s_drest, b + 1)
                        nc.scalar.activation(dot_part[1], h_dot, ACT.Copy).then_inc(s_dpart[1], 1)
                act.wait_ge(s_kb, b + 1)
                nc.scalar.activation(keybias[:, :], ps_keybias, ACT.Identity, bias=bqk[:, :]).then_inc(s_kbc, 1)
                act.wait_ge(s_kbc, b + 1)
                copy_scores(b, 0)
                for m in range(2):
                    v_part(b, m)
                for m in range(MT):
                    exponential(b, 0, m)
                    if m + 2 < MT:
                        v_part(b, m + 2)
                    p_part(b, 0, m)
                copy_scores(b, 1)
                exponential(b, 1, 0)
                for m in range(MT):
                    if m + 1 < MT:
                        exponential(b, 1, m + 1)
                    p_part(b, 1, m)
                if more:
                    for k in range(CT):
                        normed(b + 1, 1 - par, k)

            with act.Fori(0, B - 3, 2) as b:
                image(b, 0, True)
                image(b + 1, 1, True)
            image(B - 2, 0, True)
            image(B - 1, 1, False)

        @block.gpsimd
        def _(pool):
            nc.gpsimd.memset(minus_half[:, :], -0.5).then_inc(s_half, 1)
            pool.wait_ge(s_half, 1)
            pool.wait_ge(s_bb, 2)
            nc.gpsimd.partition_all_reduce(bqk[:, :], bb_sum[:, :], P, bass.bass_isa.ReduceOp.add).then_inc(s_bqk, 1)

            def inverse_deviation(n):
                pool.wait_ge(s_norm, n * NORM + 5)
                nc.gpsimd.tensor_tensor(rstd[:, :], veps[:, :], minus_half[:, :], ALU.pow).then_inc(s_rstd, 1)

            def h_part(n, k, full):
                pool.wait_ge(s_hf, n * CT + k + 1)
                pool.wait_ge(s_hhi, n * CT + k + 1)
                nc.gpsimd.tensor_tensor(h_lo[:, k, :], full, h_hi[:, k, :].bitcast(FP32),
                                        ALU.subtract).then_inc(s_hlo, 1)

            def over_partitions(b, nb, op, ready, done):
                lone_wait(pool, ready, b * 2 + nb + 1)
                nc.gpsimd.partition_all_reduce(colall[:, :], colpart[:, :], P, op).then_inc(done, 1)

            def weighted_rows(v, w, side, bias, k):
                pool.wait_ge(s_w[w][k], 2 * DMA)
                rows, by = raw[:, k, side, :], col[:, bias + k:bias + k + 1].to_broadcast([P, C])
                if k == 0:
                    nc.gpsimd.tensor_tensor(weighted[v], rows, by, ALU.mult).then_inc(s_weighted[v], 1)
                else:
                    chunk = stage[:, MT, :]
                    pool.wait_ge(s_weighted[v], k)
                    nc.gpsimd.tensor_tensor(chunk, rows, by, ALU.mult).then_inc(s_chunk[v], 1)
                    pool.wait_ge(s_chunk[v], k)
                    nc.gpsimd.tensor_tensor(weighted[v], weighted[v], chunk, ALU.add).then_inc(s_weighted[v], 1)

            pool.wait_ge(s_col, 2 * DMA)
            for k in range(CT):
                weighted_rows(1, 0, 1, BK, k)
            pool.wait_ge(s_weighted[1], CT)
            for k in range(CT - 1):
                weighted_rows(2, 1, 1, BV, k)
            inverse_deviation(0)
            weighted_rows(2, 1, 1, BV, CT - 1)
            for k in (0, 2):
                h_part(0, k, first_full[k])

            def image(b, more):
                over_partitions(b, 0, bass.bass_isa.ReduceOp.max, s_maxp, s_maxall)
                over_partitions(b, 0, bass.bass_isa.ReduceOp.add, s_sump, s_sumall)
                over_partitions(b, 1, bass.bass_isa.ReduceOp.max, s_maxp, s_maxall)
                if more:
                    inverse_deviation(b + 1)
                    for k in range(CT):
                        h_part(b + 1, k, h_full[k % 2])
                over_partitions(b, 1, bass.bass_isa.ReduceOp.add, s_sump, s_sumall)

            with pool.Fori(0, B - 1) as b:
                image(b, True)
            image(B - 1, False)

        @block.vector
        def _(dve):
            nc.vector.memset(ones[:, :], 1.0).then_inc(s_ones, 1)
            nc.vector.memset(ones_bf[:, :], 1.0).then_inc(s_ones, 1)
            dve.wait_ge(s_col, 2 * DMA)
            nc.vector.tensor_tensor(bb[:, :], col[:, BQ:BQ + CT], col[:, BK:BK + CT], ALU.mult).then_inc(s_bb, 1)
            dve.wait_ge(s_bb, 1)
            nc.vector.tensor_reduce(bb_sum[:, :], bb[:, :], AX.X, ALU.add).then_inc(s_bb, 1)

            def weight_rest(w, k):
                dve.wait_ge(s_whi, w * CT + k + 1)
                nc.vector.tensor_tensor(w_lo[w][:, 2 * k:2 * k + 2, :], raw[:, k, :, :],
                                        w_hi[w][:, 2 * k:2 * k + 2, :].bitcast(FP32), ALU.subtract).then_inc(s_wlo[w], 1)

            def weighted_rows(k):
                dve.wait_ge(s_w[0][k], 2 * DMA)
                rows, by = raw[:, k, 0, :], col[:, BQ + k:BQ + k + 1]
                if k == 0:
                    a = nc.vector.tensor_scalar(weighted[0], rows, by, None, ALU.mult)
                else:
                    dve.wait_ge(s_weighted[0], k)
                    a = nc.vector.scalar_tensor_tensor(weighted[0], rows, by, weighted[0], ALU.mult, ALU.add)
                a.then_inc(s_weighted[0], 1)

            def product_rest(w, i):
                dve.wait_ge(s_prod_hi, w * CT + product_order.index(i) + 1)
                nc.vector.tensor_tensor(product_lo[w][:, i, :], product_bank[w][i],
                                        product_hi[w][:, i, :].bitcast(FP32), ALU.subtract).then_inc(s_prod_lo, 1)

            def channel_stats(n, par, loaded=None):
                if loaded is not None:
                    dve.wait_ge(s_x[par], loaded)
                for k in range(CT):
                    if loaded is None:
                        dve.wait_ge(s_first[k], DMA)
                    for s in range(NB):
                        nc.vector.bn_stats(stats[:, k, s, :],
                                           xs[:, par, k, s * HALF:(s + 1) * HALF]).then_inc(s_stats, 1)
                lone_wait(dve, s_stats, (n + 1) * (CT * NB))
                for k in range(CT):
                    nc.vector.bn_aggr(mv[:, k, :], stats[:, k, :, :].rearrange("p s e -> p (s e)")).then_inc(s_aggr, 1)

            def about_mean(n):
                at = n * NORM
                dve.wait_ge(s_mean, n + 1)
                nc.vector.tensor_copy(gmean[:, :], ps_mean).then_inc(s_norm, 1)
                nc.vector.tensor_tensor(dmean[:, :], ps_mean, mv[:, :, 0], ALU.subtract).then_inc(s_norm, 1)
                dve.wait_ge(s_norm, at + 2)
                nc.vector.tensor_tensor(shift[:, :], dmean[:, :], dmean[:, :], ALU.mult).then_inc(s_norm, 1)
                dve.wait_ge(s_norm, at + 3)
                nc.vector.tensor_tensor(spread[:, :], shift[:, :], mv[:, :, 1], ALU.add).then_inc(s_norm, 1)

            def variance(n):
                dve.wait_ge(s_var, n + 1)
                nc.vector.tensor_scalar(veps[:, :], ps_var, EPS, None, ALU.add).then_inc(s_norm, 1)

            def affine(n, step):
                if step == 0:
                    dve.wait_ge(s_rstd, n + 1)
                    a = nc.vector.tensor_tensor(h_scale[:, :], rstd[:, :], col[:, GW:GW + CT], ALU.mult)
                else:
                    dve.wait_ge(s_norm, n * NORM + 5 + step)
                    if step == 1:
                        a = nc.vector.tensor_tensor(shift[:, :], h_scale[:, :], gmean[:, :], ALU.mult)
                    else:
                        a = nc.vector.tensor_tensor(h_bias[:, :], col[:, GB:GB + CT], shift[:, :], ALU.subtract)
                a.then_inc(s_norm, 1)

            def dot_step(n, k, full):
                dve.wait_ge(s_hf, n * CT + k + 1)
                if k == 0:
                    nc.vector.tensor_scalar(h_dot, full, k_dir[:, 0:1], None, ALU.mult).then_inc(s_hdot, 1)
                else:
                    dve.wait_ge(s_hdot, n * CT + k)
                    nc.vector.scalar_tensor_tensor(h_dot, full, k_dir[:, k:k + 1], h_dot, ALU.mult,
                                                   ALU.add).then_inc(s_hdot, 1)

            def dot_rest(n):
                dve.wait_ge(s_dpart[0], n + 1)
                nc.vector.tensor_tensor(h_dot, h_dot, dot_part[0], ALU.subtract).then_inc(s_drest, 1)

            def dot_last(n):
                dve.wait_ge(s_dpart[1], n + 1)
                nc.vector.tensor_tensor(dot_part[2], h_dot, dot_part[1], ALU.subtract).then_inc(s_dpart[2], 1)

            for k in range(CT):
                weight_rest(0, k)
                weighted_rows(k)
            channel_stats(0, 0)
            weight_rest(1, 0)
            dve.wait_ge(s_vec, 2)
            nc.vector.tensor_copy(k_dir[:, :], ps_kd).then_inc(s_vec_sb, 1)
            nc.vector.tensor_copy(t_bias[:, :], ps_tb).then_inc(s_vec_sb, 1)
            product_rest(0, product_order[0])
            dve.wait_ge(s_vec_sb, 2)
            about_mean(0)
            weight_rest(1, 1)
            variance(0)
            weight_rest(1, 2)
            for step in range(3):
                affine(0, step)

            def first_hi(k):
                dve.wait_ge(s_hf, k + 1)
                nc.vector.tensor_copy(h_hi[:, k, :], first_full[k]).then_inc(s_hhi, 1)

            def first_lo(k):
                dve.wait_ge(s_hhi, k + 1)
                nc.vector.tensor_tensor(h_lo[:, k, :], first_full[k], h_hi[:, k, :].bitcast(FP32),
                                        ALU.subtract).then_inc(s_hlo, 1)

            product_rest(0, product_order[1])
            first_hi(0)
            product_rest(0, product_order[2])
            first_hi(1)
            weight_rest(1, 3)
            first_hi(2)
            first_lo(1)
            product_rest(0, product_order[3])
            first_lo(3)
            dve.wait_ge(s_vec, 3)
            nc.vector.tensor_tensor(out_bias[:, :], ps_ob, col[:, BO:BO + CT], ALU.add).then_inc(s_vec_sb, 1)
            dve.wait_ge(s_vec_sb, 3)
            for k in range(CT):
                dot_step(0, k, first_full[k])
            for i in product_order:
                product_rest(1, i)

            def over_tiles(b, nb, first, op, ready, half_done, done):
                if first:
                    dve.wait_ge(ready, b * (2 * MT) + MT * nb + MT // 2)
                    nc.vector.tensor_reduce(stage[:, MT, :], stage[:, 0:MT // 2, :].rearrange("p s n -> p n s"),
                                            AX.X, op).then_inc(half_done, 1)
                else:
                    dve.wait_ge(ready, b * (2 * MT) + MT * (nb + 1))
                    dve.wait_ge(half_done, b * 2 + nb + 1)
                    nc.vector.tensor_reduce(colpart[:, :], stage[:, MT // 2:MT + 1, :].rearrange("p s n -> p n s"),
                                            AX.X, op).then_inc(done, 1)

            def key_max(b, nb, first):
                over_tiles(b, nb, first, ALU.max, s_copied, s_maxh, s_maxp)

            def key_sum(b, nb, first):
                over_tiles(b, nb, first, ALU.add, s_exp, s_sumh, s_sump)

            def subtract_max(b, nb, m):
                if m == 0:
                    dve.wait_ge(s_maxall, b * 2 + nb + 1)
                nc.vector.tensor_tensor(stage[:, m, :], stage[:, m, :], colall[:, :], ALU.subtract).then_inc(s_sub, 1)

            def p_rest(b, nb, m):
                dve.wait_ge(s_phi, b * (2 * MT) + MT * nb + m + 1)
                nc.vector.tensor_tensor(p_lo[:, m, :], stage[:, m, :], p_hi[:, m, :].bitcast(FP32),
                                        ALU.subtract).then_inc(s_plo, 1)

            def v_rest(b, m):
                dve.wait_ge(s_vhi, b * 8 + m + 1)
                nc.vector.tensor_tensor(v_lo[:, m, :], ring[:, (V0 + m) % RING, :], v_hi[:, m, :].bitcast(FP32),
                                        ALU.subtract).then_inc(s_vlo, 1)

            def inverse(b, nb):
                dve.wait_ge(s_sumall, b * 2 + nb + 1)
                nc.vector.reciprocal(inv[:, :], colall[:, :]).then_inc(s_inv, 1)

            def scale_output(b, nb, c):
                dve.wait_ge(s_inv, b * 2 + nb + 1)
                dve.wait_ge(s_bank, b * (2 * CT) + CT * nb + c + 1)
                if nb == 0 and c == 3:
                    dve.wait_ge(s_sub, b * (2 * MT) + 2 * MT)
                nc.vector.tensor_tensor(scaled_at[c], av[:, c, :], inv[:, :], ALU.mult).then_inc(s_scaled, 1)

            def add_input(b, par, nb, c):
                dve.wait_ge(s_scaled, b * (2 * CT) + CT * nb + c + 1)
                here = xs[:, par, c, nb * HALF:(nb + 1) * HALF]
                nc.vector.scalar_tensor_tensor(here, scaled_at[c], out_bias[:, c:c + 1], here, ALU.add,
                                               ALU.add).then_inc(s_result, 1)

            def image(b, par, more):
                for j in range(NB * CT):
                    half, i = j // CT, j % CT
                    here = slice(half * HALF, (half + 1) * HALF)
                    dve.wait_ge(s_thi, b * 8 + j + 1)
                    nc.vector.scalar_tensor_tensor(t_lo[:, i, here], ring[:, (T0 + j) % RING, :], t_bias[:, i:i + 1],
                                                   t_hi[:, i, here].bitcast(FP32), ALU.add,
                                                   ALU.subtract).then_inc(s_tlo, 1)
                    if j == 1:
                        dot_rest(b)
                    if j == 3:
                        dot_last(b)
                key_max(b, 0, True)
                key_max(b, 0, False)
                for m in range(2):
                    v_rest(b, m)
                for m in range(MT):
                    subtract_max(b, 0, m)
                    if m >= 1:
                        p_rest(b, 0, m - 1)
                    if m + 2 < MT:
                        v_rest(b, m + 2)
                    if m == MT // 2:
                        key_sum(b, 0, True)
                p_rest(b, 0, MT - 1)
                key_sum(b, 0, False)
                dve.wait_ge(s_sump, b * 2 + 1)
                key_max(b, 1, True)
                inverse(b, 0)
                if more:
                    channel_stats(b + 1, 1 - par, (b - par) * (DMA // 2) + DMA)
                key_max(b, 1, False)
                if more:
                    about_mean(b + 1)
                subtract_max(b, 1, 0)
                subtract_max(b, 1, 1)
                for m in range(2, MT):
                    subtract_max(b, 1, m)
                    if more and m >= MT - 2:
                        affine(b + 1, 2 * (m - MT + 2))
                    if m < MT - 1:
                        p_rest(b, 1, m - 2)
                    if more and m == MT - 2:
                        affine(b + 1, 1)
                    if more and m == 4:
                        variance(b + 1)
                key_sum(b, 1, True)
                for c in range(CT):
                    scale_output(b, 0, c)
                for c in range(CT):
                    add_input(b, par, 0, c)
                p_rest(b, 1, MT - 3)
                dve.wait_ge(s_result, b * (2 * CT) + CT)
                key_sum(b, 1, False)
                if more:
                    dve.wait_ge(s_sump, b * 2 + 2)
                    dve.wait_ge(s_plo, b * (2 * MT) + 2 * MT - 2)
                    dot_step(b + 1, 0, h_full[0])
                    dot_step(b + 1, 1, h_full[1])
                p_rest(b, 1, MT - 2)
                p_rest(b, 1, MT - 1)
                if more:
                    dot_step(b + 1, 2, h_full[0])
                    dot_step(b + 1, 3, h_full[1])
                inverse(b, 1)
                if more:
                    for c in range(CT):
                        scale_output(b, 1, c)
                    for c in range(CT):
                        add_input(b, par, 1, c)
                else:
                    for c in range(CT):
                        scale_output(b, 1, c)
                        add_input(b, par, 1, c)

            with dve.Fori(0, B - 3, 2) as b:
                image(b, 0, True)
                image(b + 1, 1, True)
            image(B - 2, 0, True)
            image(B - 1, 1, False)


def kernel(x, L0_conv_gn_w, L0_conv_gn_b, L0_conv_qkv_w, L0_conv_qkv_b, L0_conv_out_w, L0_conv_out_b):
    import concourse.bacc as bacc
    from concourse.bass_utils import run_bass_kernel_spmd

    rows = np.concatenate([np.asarray(a).reshape(-1, P) for a in
                           (L0_conv_qkv_b, L0_conv_gn_w, L0_conv_gn_b, L0_conv_out_b)])
    arrays = {
        "x_in": np.ascontiguousarray(x).reshape(B, C, N),
        "wq": np.ascontiguousarray(L0_conv_qkv_w[0:C]),
        "wk": np.ascontiguousarray(L0_conv_qkv_w[C:2 * C]),
        "wv": np.ascontiguousarray(L0_conv_qkv_w[2 * C:3 * C]),
        "wo_t": np.ascontiguousarray(np.asarray(L0_conv_out_w).T),
        "cols": np.ascontiguousarray(rows.T),
        "block_avg": np.kron(np.eye(P * GROUPS // C), np.full((C // GROUPS,) * 2, GROUPS / C)).astype(np.float32),
    }
    nc = bacc.Bacc("TRN2", target_bir_lowering=False, num_devices=1, dynamic_dma_scratch_size=1024)
    ins = [nc.dram_tensor(n, a.shape, mybir.dt.from_np(a.dtype), kind="ExternalInput").ap() for n, a in arrays.items()]
    out = nc.dram_tensor("out", (B, C, N), FP32, kind="ExternalOutput").ap()
    attention_kernel(nc, *ins, out)
    r = run_bass_kernel_spmd(nc, [arrays], core_ids=[0])
    return r.results[0]["out"].reshape(B, C, H, W)
```
